# Optimizing a Trainium2 kernel written in Bass

```python
import numpy as np
import jax
import jax.numpy as jnp

def _softmax(x, axis=-1):
    return jax.nn.softmax(x, axis=axis)

def _gelu(x):
    return jax.nn.gelu(x, approximate=True)

def _silu(x):
    return jax.nn.silu(x)

def _sigmoid(x):
    return jax.nn.sigmoid(x)

def _layernorm(x, axis=-1, eps=1e-05):
    m = jnp.mean(x, axis=axis, keepdims=True)
    v = jnp.var(x, axis=axis, keepdims=True)
    return (x - m) / jnp.sqrt(v + eps)

def _scatter_add(tgt, idx, src, axis=0):
    return tgt.at[idx].add(src)

def _segment_sum(src, seg, n):
    return jax.ops.segment_sum(src, seg, n)
kernel_name = 'mk_audio_tower_d1_tok_audfeat2048_r4_dbf379'

def setup_inputs(seed: int=0):
    np.random.seed(seed)
    _w = jnp.asarray

    def _rec_inputs():
        import jax
        import jax.numpy as jnp
        _rk = jax.random.key(seed)
        x = -0.000392918 + 0.999932 * jax.random.normal(jax.random.fold_in(_rk, 1), (64, 125, 64), jnp.float32)
        return x
    x = _rec_inputs()

    def _L0_tok_setup():
        import jax, jax.numpy as jnp
        import numpy as np
        TIN = 16
        FEAT = 64
        IN_DIM = TIN * FEAT
        HDIM = 512
        EPS = 1e-06

        def layer_norm(x, gamma, beta, eps):
            mu = jnp.mean(x, axis=-1, keepdims=True)
            var = jnp.mean(jnp.square(x - mu), axis=-1, keepdims=True)
            return (x - mu) * jax.lax.rsqrt(var + eps) * gamma + beta
        key = jax.random.key(seed)
        ks = jax.random.split(key, 4)
        x = jax.random.normal(ks[0], (64, 1024, FEAT), dtype=jnp.float32)
        W = jax.random.normal(ks[1], (IN_DIM, HDIM), dtype=jnp.float32) / np.sqrt(IN_DIM)
        b = jnp.zeros((HDIM,), dtype=jnp.float32)
        g1 = jnp.ones((IN_DIM,), dtype=jnp.float32)
        b1 = jnp.zeros((IN_DIM,), dtype=jnp.float32)
        g2 = jnp.ones((HDIM,), dtype=jnp.float32)
        b2 = jnp.zeros((HDIM,), dtype=jnp.float32)
        return {'x': x, 'W': W, 'b': b, 'g1': g1, 'b1': b1, 'g2': g2, 'b2': b2}
    _L0_tok_all = _L0_tok_setup()
    _L0_tok_in = {k: v for k, v in _L0_tok_all.items() if k in ('W', 'b', 'g1', 'b1', 'g2', 'b2')}
    del _L0_tok_all

    def _L0_attn_setup():
        import jax, jax.numpy as jnp
        import numpy as np
        import math
        D_MODEL = 512
        N_HEADS = 16
        D_HEAD = 128
        BATCH = 2
        SEQ = 512
        key = jax.random.key(seed)
        ks = jax.random.split(key, 5)
        std = 0.02
        x = jax.random.normal(ks[0], (BATCH, SEQ, D_MODEL), dtype=jnp.float32)
        W_Q = std * jax.random.normal(ks[1], (N_HEADS, D_HEAD, D_MODEL), dtype=jnp.float32)
        W_K = std * jax.random.normal(ks[2], (N_HEADS, D_HEAD, D_MODEL), dtype=jnp.float32)
        W_V = std * jax.random.normal(ks[3], (N_HEADS, D_HEAD, D_MODEL), dtype=jnp.float32)
        W_O = std * jax.random.normal(ks[4], (N_HEADS, D_MODEL, D_HEAD), dtype=jnp.float32)
        return {'x': x, 'W_Q': W_Q, 'W_K': W_K, 'W_V': W_V, 'W_O': W_O}
    _L0_attn_all = _L0_attn_setup()
    _L0_attn_in = {k: v for k, v in _L0_attn_all.items() if k in ('W_Q', 'W_K', 'W_V', 'W_O')}
    del _L0_attn_all

    def _L0_ffn_setup():
        import jax, jax.numpy as jnp
        import numpy as np
        FP8_MAX = 448.0
        SCALE_EPS = 1e-07
        key = jax.random.key(seed)
        k1, k2, k3 = jax.random.split(key, 3)
        in_f, out_f = (512, 512)
        x = jax.random.normal(k1, (4, 1024, in_f), dtype=jnp.float32)
        w_fp32 = jax.random.normal(k2, (out_f, in_f), dtype=jnp.float32) * (1.0 / np.sqrt(in_f))
        weight = w_fp32.astype(jnp.float8_e4m3fn).astype(jnp.float32)
        weight_scale = jnp.ones((), dtype=jnp.float32)
        bound = 1.0 / np.sqrt(in_f)
        bias = jax.random.uniform(k3, (out_f,), dtype=jnp.float32, minval=-bound, maxval=bound)
        return {'x': x, 'weight': weight, 'weight_scale': weight_scale, 'bias': bias}
    _L0_ffn_all = _L0_ffn_setup()
    _L0_ffn_in = {k: v for k, v in _L0_ffn_all.items() if k in ('weight', 'weight_scale', 'bias')}
    del _L0_ffn_all
    return {'x': x, 'L0_tok_W': _L0_tok_in['W'], 'L0_tok_b': _L0_tok_in['b'], 'L0_tok_g1': _L0_tok_in['g1'], 'L0_tok_b1': _L0_tok_in['b1'], 'L0_tok_g2': _L0_tok_in['g2'], 'L0_tok_b2': _L0_tok_in['b2'], 'L0_attn_W_Q': _L0_attn_in['W_Q'], 'L0_attn_W_K': _L0_attn_in['W_K'], 'L0_attn_W_V': _L0_attn_in['W_V'], 'L0_attn_W_O': _L0_attn_in['W_O'], 'L0_ffn_weight': _L0_ffn_in['weight'], 'L0_ffn_weight_scale': _L0_ffn_in['weight_scale'], 'L0_ffn_bias': _L0_ffn_in['bias']}

def reference(x, L0_tok_W, L0_tok_b, L0_tok_g1, L0_tok_b1, L0_tok_g2, L0_tok_b2, L0_attn_W_Q, L0_attn_W_K, L0_attn_W_V, L0_attn_W_O, L0_ffn_weight, L0_ffn_weight_scale, L0_ffn_bias):
    import jax
    import jax.numpy as jnp

    def _L0_tok_ref(x, W, b, g1, b1, g2, b2):
        import jax, jax.numpy as jnp
        import numpy as np
        TIN = 16
        FEAT = 64
        IN_DIM = TIN * FEAT
        HDIM = 512
        EPS = 1e-06

        def layer_norm(x, gamma, beta, eps):
            mu = jnp.mean(x, axis=-1, keepdims=True)
            var = jnp.mean(jnp.square(x - mu), axis=-1, keepdims=True)
            return (x - mu) * jax.lax.rsqrt(var + eps) * gamma + beta
        bsz, T, F = x.shape
        n_patch = T // TIN
        x = x[:, :n_patch * TIN, :].reshape(bsz, n_patch, TIN * F)
        x = layer_norm(x, g1, b1, EPS)
        x = jnp.einsum('bpd,dh->bph', x, W) + b
        return layer_norm(x, g2, b2, EPS)

    def _L0_attn_ref(x, W_Q, W_K, W_V, W_O):
        import jax, jax.numpy as jnp
        import numpy as np
        import math
        D_MODEL = 512
        N_HEADS = 16
        D_HEAD = 128
        BATCH = 2
        SEQ = 512
        d_head = W_Q.shape[1]
        seq_len = x.shape[1]
        scale = 1.0 / math.sqrt(d_head)
        q = jnp.einsum('bsd,hed->bhse', x, W_Q)
        k = jnp.einsum('bsd,hed->bhse', x, W_K)
        v = jnp.einsum('bsd,hed->bhse', x, W_V)
        scores = jnp.einsum('bhse,bhme->bhsm', q, k) * scale
        causal = jnp.triu(jnp.ones((seq_len, seq_len), dtype=bool), k=1)
        scores = jnp.where(causal, jnp.float32(-1000000000.0), scores)
        pattern = jax.nn.softmax(scores, axis=-1)
        z = jnp.einsum('bhsm,bhme->bhse', pattern, v)
        out = jnp.einsum('bhse,hde->bsd', z, W_O)
        return out

    def _L0_ffn_ref(x, weight, weight_scale, bias):
        import jax, jax.numpy as jnp
        import numpy as np
        FP8_MAX = 448.0
        SCALE_EPS = 1e-07
        scale = jnp.maximum(jnp.max(jnp.abs(x)) / FP8_MAX, SCALE_EPS)
        x_q = (x / scale).astype(jnp.float8_e4m3fn).astype(jnp.float32)
        w = weight * weight_scale
        out = jnp.einsum('bsi,oi->bso', x_q, w) + bias
        return out
    h = _L0_tok_ref(x, L0_tok_W, L0_tok_b, L0_tok_g1, L0_tok_b1, L0_tok_g2, L0_tok_b2)
    h = h + _L0_attn_ref(_layernorm(h, axis=-1), L0_attn_W_Q, L0_attn_W_K, L0_attn_W_V, L0_attn_W_O)
    h = h + _L0_ffn_ref(_layernorm(h, axis=-1), L0_ffn_weight, L0_ffn_weight_scale, L0_ffn_bias)
    return h

_drawn_inputs = setup_inputs


def setup_inputs(seed=0):
    import zlib

    import numpy as np

    out = dict(_drawn_inputs(seed))
    spreads = {'L0_tok_b': (0.0, 0.1),
     'L0_tok_g1': (1.0, 0.2),
     'L0_tok_b1': (0.0, 0.1),
     'L0_tok_g2': (1.0, 0.2),
     'L0_tok_b2': (0.0, 0.1)}
    factors = {'L0_ffn_bias': 64.0}
    for name, (base, spread) in spreads.items():
        noise = np.random.default_rng([zlib.crc32(name.encode()), seed]).standard_normal(out[name].shape)
        drawn = base * np.exp(spread * noise) if base else spread * noise
        out[name] = jnp.asarray(drawn.astype(out[name].dtype))
    for name, factor in factors.items():
        out[name] = (out[name] * factor).astype(out[name].dtype)
    return out
```

```python
import math
from contextlib import ExitStack

import concourse.bass as bass
from concourse import mybir

ALU = mybir.AluOpType
ACT = mybir.ActivationFunctionType
AX = mybir.AxisListType
F32 = mybir.dt.float32
F32R = mybir.dt.float32r
I32 = mybir.dt.int32

BATCH, PATCHES = 64, 7
ROWS = BATCH * PATCHES
IN_DIM = 1024
D = 512
HEADS, E = 16, 128
TILES = 4
TR = ROWS // TILES
KIN = IN_DIM // 128
KD = D // 128
QKV = 3 * KD * E
WCOLS = QKV + D
SCALE = 1.0 / math.sqrt(E)
LN_EPS, NORM_EPS = 1e-6, 1e-5
FP8_MAX, SCALE_EPS = 448.0, 1e-7
EXP_MASK = 0x7F800000
FP8_MIN_NORMAL = 2.0 ** -6
ROUND_TO_4_BITS = 1.5 * 2.0 ** 20
RSQRT_SEED = float(0x5F3759DF)
NEWTON_STEPS = 3


def audio_tower(nc, patches, tok_w, heads_w, ffn_w, tok_g1, tok_b1, tok_b, tok_g2, tok_b2,
                ffn_scale, ffn_bias, mask, ident, out):
    with ExitStack() as ctx:
        def sb(name, shape, dt=F32):
            return ctx.enter_context(nc.sbuf_tensor(name, shape, dt))

        def sem(name):
            return ctx.enter_context(nc.semaphore(name))

        ident_sb = sb("ident_sb", [128, 128])
        mask_sb = sb("mask_sb", [TR, TILES * TR])
        g1_col = sb("g1_col", [128, KIN])
        b1_col = sb("b1_col", [128, KIN])
        tok_b_row = sb("tok_b_row", [TR, D])
        g2_row = sb("g2_row", [TR, D])
        b2_row = sb("b2_row", [TR, D])
        ffn_b_row = sb("ffn_b_row", [TR, D])
        ffn_scale_col = sb("ffn_scale_col", [128, 1])

        x_in = sb("x_in", [TR, TILES, IN_DIM])
        tokw_raw = sb("tokw_raw", [128, KIN, D])
        tokw_hi = sb("tokw_hi", [128, KIN, D], F32R)
        tokw_lo = sb("tokw_lo", [128, KIN, D], F32R)
        xt = sb("xt", [128, 2, KIN * TR])
        xt_hi = sb("xt_hi", [128, 2, KIN * TR], F32R)
        xt_lo = sb("xt_lo", [128, 2, KIN * TR], F32R)

        h_sb = sb("h_sb", [TR, TILES, D])
        hn_sb = sb("hn_sb", [TR, TILES, D])
        ht_hi = sb("ht_hi", [128, KD, ROWS], F32R)
        ht_lo = sb("ht_lo", [128, KD, ROWS], F32R)

        raw = sb("raw", [128, 2, WCOLS])
        qkvw_hi = [sb(f"qkvw_hi{s}", [128, 3, KD, E], F32R) for s in range(2)]
        qkvw_lo = [sb(f"qkvw_lo{s}", [128, 3, KD, E], F32R) for s in range(2)]
        outw_hi = [sb(f"outw_hi{s}", [128, D], F32R) for s in range(2)]
        outw_lo = [sb(f"outw_lo{s}", [128, D], F32R) for s in range(2)]

        q_t = sb("q_t", [128, ROWS])
        k_t = sb("k_t", [128, ROWS])
        v_t = sb("v_t", [128, ROWS])
        v_nat = sb("v_nat", [TR, TILES, E])
        prob = sb("prob", [TR, TILES, TR])
        prob_t = sb("prob_t", [TR, TILES, TR])
        z_hi = sb("z_hi", [128, TILES, TR], F32R)
        z_lo = sb("z_lo", [128, TILES, TR], F32R)
        smax = sb("smax", [TR, TILES])
        ssum = sb("ssum", [TR, TILES])
        srec = sb("srec", [TR, TILES])

        ffnw_raw, ffnw_hi, ffnw_lo = tokw_raw[:, 0:KD, :], tokw_hi[:, 0:KD, :], tokw_lo[:, 0:KD, :]
        xq_bits = x_in[:, :, 0:D]
        y_sb = x_in[:, :, D:2 * D]
        xq_t = xt_hi[:].rearrange("p a (b c) -> p (a b) c", b=2)

        stats = sb("stats", [TR, TILES, 2, 6])
        moments = sb("moments", [TR, TILES, 2])
        veps = sb("veps", [TR, TILES])
        rstd = sb("rstd", [TR, TILES])
        nmr = sb("nmr", [TR, TILES])
        newton = sb("newton", [TR, 2, TILES])
        ones_row = sb("ones_row", [1, TR])
        tile_max = sb("tile_max", [TR, TILES])
        row_max = sb("row_max", [TR, 1])
        q_scale = sb("q_scale", [1, 2])
        inv_scale = sb("inv_scale", [TR, 1])

        bank = [ctx.enter_context(nc.psum_tensor(f"bank{i}", [128, 512], F32)) for i in range(4)]
        acc = [ctx.enter_context(nc.psum_tensor(f"acc{t}", [128, D], F32)) for t in range(TILES)]

        const_in = sem("const_in")
        x_landed = [sem(f"x_landed{t}") for t in range(TILES)]
        tokw_landed = [sem(f"tokw_landed{i}") for i in range(2)]
        raw_landed = [sem(f"raw_landed{s}") for s in range(2)]
        ffnw_landed = sem("ffnw_landed")
        out_stored = sem("out_stored")

        dve_step = sem("dve_step")
        x_scaled = sem("x_scaled")
        x_normed = sem("x_normed")
        xt_ps = sem("xt_ps")
        xt_evac_a = sem("xt_evac_a")
        xt_evac_v = sem("xt_evac_v")
        xt_hi_ok = sem("xt_hi_ok")
        xt_lo_ok = sem("xt_lo_ok")
        tokw_hi_ok = sem("tokw_hi_ok")
        tokw_lo_ok = sem("tokw_lo_ok")
        tok_ps = sem("tok_ps")
        h_ok = sem("h_ok")
        hn_ok = sem("hn_ok")
        ht_ps = sem("ht_ps")
        ht_hi_ok = sem("ht_hi_ok")
        ht_lo_ok = sem("ht_lo_ok")

        qkvw_hi_ok = sem("qkvw_hi_ok")
        qkvw_lo_ok = sem("qkvw_lo_ok")
        outw_hi_ok = sem("outw_hi_ok")
        outw_lo_ok = sem("outw_lo_ok")
        q_ps, k_ps, v_ps = sem("q_ps"), sem("k_ps"), sem("v_ps")
        q_ok, k_ok, vt_ok = sem("q_ok"), sem("k_ok"), sem("vt_ok")
        s_ps = sem("s_ps")
        s_read = sem("s_read")
        shifted = sem("shifted")
        exp_ok = sem("exp_ok")
        prob_ok = sem("prob_ok")
        pt_ps, pt_ok = sem("pt_ps"), sem("pt_ok")
        vn_ps, vn_ok = sem("vn_ps"), sem("vn_ok")
        z_ps, z_hi_ok, z_lo_ok = sem("z_ps"), sem("z_hi_ok"), sem("z_lo_ok")
        o_ps = sem("o_ps")
        softmax_step = sem("softmax_step")

        ffnw_hi_ok = sem("ffnw_hi_ok")
        ffnw_lo_ok = sem("ffnw_lo_ok")
        ones_ok = sem("ones_ok")
        max_ok = sem("max_ok")
        max_ps = sem("max_ps")
        scale_ok = sem("scale_ok")
        scale_ps = sem("scale_ps")
        xq_ok = sem("xq_ok")
        xqt_ps = sem("xqt_ps")
        xqt_ok = sem("xqt_ok")
        y_ps = sem("y_ps")
        y_ok = sem("y_ok")

        N_CONST = 9
        block = ctx.enter_context(nc.Block())

        def loop_heads(eng, step):
            with eng.Fori(0, (HEADS - 2) // 2) as i:
                step(i * 2 + 1, i, 1)
                step(i * 2 + 2, i + 1, 0)

        @block.sync
        def _(sp):
            sp.dma_start(x_in[:, 0, :], patches[0]).then_inc(x_landed[0], 16)
            sp.dma_start(ident_sb[:], ident).then_inc(const_in, 16)
            sp.dma_start(g1_col[:], tok_g1).then_inc(const_in, 16)
            sp.dma_start(b1_col[:], tok_b1).then_inc(const_in, 16)
            for i in range(2):
                k = slice(i * KIN // 2, (i + 1) * KIN // 2)
                sp.dma_start(tokw_raw[:, k, :], tok_w[:, k, :]).then_inc(tokw_landed[i], 16)
                sp.dma_start(x_in[:, i + 1, :], patches[i + 1]).then_inc(x_landed[i + 1], 16)
            sp.dma_start(x_in[:, 3, :], patches[3]).then_inc(x_landed[3], 16)
            for dst, src in ((tok_b_row, tok_b), (g2_row, tok_g2), (b2_row, tok_b2), (ffn_b_row, ffn_bias)):
                sp.dma_start(dst[:], src.to_broadcast([TR, D])).then_inc(const_in, 16)
            sp.dma_start(mask_sb[:], mask).then_inc(const_in, 16)
            sp.dma_start(ffn_scale_col[:], ffn_scale.to_broadcast([128, 1])).then_inc(const_in, 16)
            for s in range(2):
                sp.dma_start(raw[:, s, :], heads_w[s]).then_inc(raw_landed[s], 16)
            sp.wait_ge(tokw_lo_ok, KIN)
            sp.dma_start(ffnw_raw, ffn_w).then_inc(ffnw_landed, 16)

            def load_head(h, _, s):
                sp.wait_ge(outw_hi_ok, h)
                sp.wait_ge(outw_lo_ok, h)
                sp.dma_start(raw[:, 1 - s, :], heads_w[h + 1]).then_inc(raw_landed[1 - s], 16)

            loop_heads(sp, load_head)
            for t in range(TILES):
                sp.wait_ge(y_ok, t + 1)
                sp.dma_start(out[t], y_sb[:, t, :]).then_inc(out_stored, 16)
            sp.wait_ge(out_stored, 16 * TILES)

        @block.tensor
        def _(pe):
            def split_product(ps, hi, lo, whi, wlo, first, last):
                nc.tensor.matmul(ps, hi, whi, start=first, stop=False, skip_group_check=True)
                nc.tensor.matmul(ps, hi, wlo, start=False, stop=False, skip_group_check=True)
                return nc.tensor.matmul(ps, lo, whi, start=False, stop=last, skip_group_check=True)

            def patch_transposes(t):
                pe.wait_ge(x_normed, t + 1)
                if t == 0:
                    pe.wait_ge(const_in, 16 * N_CONST)
                if t >= 2:
                    pe.wait_ge(xt_evac_a, t - 1)
                    pe.wait_ge(xt_evac_v, t - 1)
                for k in range(KIN):
                    b = 2 * (t % 2) + k // 4
                    last = nc.tensor.transpose(bank[b][:, k % 4 * TR:(k % 4 + 1) * TR],
                                               x_in[:, t, k * 128:(k + 1) * 128], ident_sb[0:TR, 0:TR])
                last.then_inc(xt_ps, 1)

            def embed(t):
                pe.wait_ge(xt_hi_ok, t + 1)
                pe.wait_ge(xt_lo_ok, t + 1)
                for k in range(KIN):
                    if t == 0:
                        pe.wait_ge(tokw_hi_ok, k + 1)
                        pe.wait_ge(tokw_lo_ok, k + 1)
                    c = slice(k * TR, (k + 1) * TR)
                    last = split_product(acc[t][0:TR, :], xt_hi[:, t % 2, c], xt_lo[:, t % 2, c],
                                         tokw_hi[:, k, :], tokw_lo[:, k, :], k == 0, k == KIN - 1)
                last.then_inc(tok_ps, 1)

            def stream_transposes(t):
                pe.wait_ge(hn_ok, t + 1)
                if t == 0:
                    pe.wait_ge(xt_evac_a, TILES)
                    pe.wait_ge(xt_evac_v, TILES)
                for k in range(KD):
                    last = nc.tensor.transpose(bank[t][:, k * TR:(k + 1) * TR],
                                               hn_sb[:, t, k * 128:(k + 1) * 128], ident_sb[0:TR, 0:TR])
                last.then_inc(ht_ps, 1)

            def seed(t):
                pe.wait_ge(h_ok, t + 1)
                mm = nc.tensor.matmul(acc[t][0:TR, :], ident_sb[0:TR, 0:TR], h_sb[:, t, :],
                                      start=True, stop=False, skip_group_check=True)
                if t == TILES - 1:
                    mm.then_inc(o_ps, 1)

            patch_transposes(0)
            for t in range(TILES):
                if t + 1 < TILES:
                    patch_transposes(t + 1)
                embed(t)
            for t in range(TILES):
                stream_transposes(t)
                seed(t)

            def project(which, ps, s, done):
                for k in range(KD):
                    wh, wl = qkvw_hi[s][:, which, k, :], qkvw_lo[s][:, which, k, :]
                    last = split_product(ps[:, 0:ROWS], wh, wl, ht_hi[:, k, :], ht_lo[:, k, :],
                                         k == 0, k == KD - 1)
                last.then_inc(done, 1)

            def project_q(h, s):
                pe.wait_ge(qkvw_hi_ok, h + 1)
                pe.wait_ge(qkvw_lo_ok, h + 1)
                project(0, bank[0], s, q_ps)

            def project_v(h, s):
                pe.wait_ge(q_ok, h + 1)
                project(2, bank[0], s, v_ps)

            def prob_transposes(h):
                pe.wait_ge(prob_ok, h + 1)
                pe.wait_ge(vn_ok, h + 1)
                for t in range(TILES):
                    last = nc.tensor.transpose(bank[3][0:TR, t * TR:(t + 1) * TR], prob[:, t, :],
                                               ident_sb[0:TR, 0:TR])
                last.then_inc(pt_ps, 1)

            def weigh_values(h):
                pe.wait_ge(pt_ok, h + 1)
                for t in range(TILES):
                    last = nc.tensor.matmul(bank[2][:, t * TR:(t + 1) * TR], v_nat[:, t, :],
                                            prob_t[:, t, :], start=True, stop=True)
                last.then_inc(z_ps, 1)

            def scores(h):
                pe.wait_ge(k_ok, h + 1)
                for t in range(TILES):
                    c = slice(t * TR, (t + 1) * TR)
                    last = nc.tensor.matmul(bank[1][0:TR, c], q_t[:, c], k_t[:, c], start=True, stop=True)
                last.then_inc(s_ps, 1)

            def value_transposes(h):
                pe.wait_ge(vt_ok, h + 1)
                for t in range(TILES):
                    last = nc.tensor.transpose(bank[3][0:TR, t * E:(t + 1) * E],
                                               v_t[:, t * TR:(t + 1) * TR], ident_sb[:])
                last.then_inc(vn_ps, 1)

            def project_out(h, s, final=False):
                pe.wait_ge(outw_hi_ok, h + 1)
                pe.wait_ge(outw_lo_ok, h + 1)
                pe.wait_ge(z_hi_ok, h + 1)
                if not final:
                    for t in range(TILES):
                        for w in (outw_hi[s], outw_lo[s]):
                            nc.tensor.matmul(acc[t][0:TR, :], z_hi[:, t, :], w[:], start=False, stop=False,
                                             skip_group_check=True)
                    pe.wait_ge(z_lo_ok, h + 1)
                    for t in range(TILES):
                        last = nc.tensor.matmul(acc[t][0:TR, :], z_lo[:, t, :], outw_hi[s][:], start=False,
                                                stop=False, skip_group_check=True)
                    last.then_inc(o_ps, 1)
                else:
                    pe.wait_ge(z_lo_ok, h + 1)
                    for t in range(TILES):
                        split_product(acc[t][0:TR, :], z_hi[:, t, :], z_lo[:, t, :], outw_hi[s][:],
                                      outw_lo[s][:], False, True).then_inc(o_ps, 1)

            def head_step(h, _, s, first=False):
                project_q(h, s)
                if not first:
                    pe.wait_ge(s_read, h)
                project(1, bank[1], s, k_ps)
                if not first:
                    prob_transposes(h - 1)
                project_v(h, s)
                if not first:
                    weigh_values(h - 1)
                scores(h)
                value_transposes(h)
                if not first:
                    project_out(h - 1, 1 - s)

            pe.wait_ge(ht_hi_ok, TILES)
            pe.wait_ge(ht_lo_ok, TILES)
            head_step(0, 0, 0, first=True)
            loop_heads(pe, head_step)
            head_step(HEADS - 1, None, 1)
            prob_transposes(HEADS - 1)
            weigh_values(HEADS - 1)
            project_out(HEADS - 1, 1, final=True)

            pe.wait_ge(max_ok, 1)
            nc.tensor.transpose(bank[0][0:1, 0:TR], row_max[:], ident_sb[0:TR, 0:TR]).then_inc(max_ps, 1)
            pe.wait_ge(ones_ok, 1)
            pe.wait_ge(scale_ok, 1)
            nc.tensor.matmul(bank[1][0:TR, 0:1], ones_row[:], q_scale[:, 1:2], start=True,
                             stop=True).then_inc(scale_ps, 1)
            pe.wait_ge(ffnw_hi_ok, 1)
            pe.wait_ge(ffnw_lo_ok, 1)

            def quantised_transposes(t):
                pe.wait_ge(xq_ok, t + 1)
                for k in range(KD):
                    last = nc.tensor.transpose(bank[(t + 2) % 4][:, k * TR:(k + 1) * TR],
                                               hn_sb[:, t, k * 128:(k + 1) * 128], ident_sb[0:TR, 0:TR])
                last.then_inc(xqt_ps, 1)

            def feed_forward(t):
                pe.wait_ge(xqt_ok, t + 1)
                for k in range(KD):
                    for w in (ffnw_hi, ffnw_lo):
                        last = nc.tensor.matmul(acc[t][0:TR, :], xq_t[:, t, k * TR:(k + 1) * TR], w[:, k, :],
                                                start=(k == 0 and w is ffnw_hi),
                                                stop=(k == KD - 1 and w is ffnw_lo))
                last.then_inc(y_ps, 1)

            for t in range(TILES):
                quantised_transposes(t)
                if t >= 1:
                    feed_forward(t - 1)
            feed_forward(TILES - 1)

        @block.scalar
        def _(act):
            def hi_part(dst, src):
                return nc.scalar.copy(dst, src)

            def normalise(t):
                act.wait_ge(x_scaled, t + 1)
                nc.scalar.activation(x_in[:, t, :], x_in[:, t, :], ACT.Identity, bias=nmr[:, t:t + 1],
                                     scale=rstd[:, t:t + 1]).then_inc(x_normed, 1)

            def patch_evacuate(t):
                act.wait_ge(xt_ps, t + 1)
                if t >= 2:
                    act.wait_ge(xt_hi_ok, t - 1)
                    act.wait_ge(xt_lo_ok, t - 1)
                for k in range(KIN // 2):
                    last = nc.scalar.activation(xt[:, t % 2, k * TR:(k + 1) * TR],
                                                bank[2 * (t % 2)][:, k * TR:(k + 1) * TR], ACT.Identity,
                                                bias=b1_col[:, k:k + 1], scale=g1_col[:, k:k + 1])
                last.then_inc(xt_evac_a, 1)
                act.wait_ge(xt_evac_a, t + 1)
                act.wait_ge(xt_evac_v, t + 1)
                if t >= 2:
                    act.wait_ge(tok_ps, t - 1)
                hi_part(xt_hi[:, t % 2, :], xt[:, t % 2, :]).then_inc(xt_hi_ok, 1)

            def stream_evacuate(t):
                act.wait_ge(ht_ps, t + 1)
                hi_part(ht_hi[:, :, t * TR:(t + 1) * TR],
                        bank[t][:, 0:KD * TR].rearrange("p (k r) -> p k r", k=KD)).then_inc(ht_hi_ok, 1)

            normalise(0)
            act.wait_ge(const_in, 16 * N_CONST)
            for k in range(KIN):
                act.wait_ge(tokw_landed[2 * k // KIN], 16)
                hi_part(tokw_hi[:, k, :], tokw_raw[:, k, :]).then_inc(tokw_hi_ok, 1)
                if k == 1:
                    patch_evacuate(0)
            for t in range(1, TILES):
                normalise(t)
                patch_evacuate(t)

            def split_qkv(h, r, s):
                act.wait_ge(raw_landed[s], (r + 1) * 16)
                hi_part(qkvw_hi[s][:].rearrange("p a k e -> p (a k e)"),
                        raw[:, s, 0:QKV]).then_inc(qkvw_hi_ok, 1)

            def split_out(h, s):
                hi_part(outw_hi[s][:], raw[:, s, QKV:WCOLS]).then_inc(outw_hi_ok, 1)

            split_qkv(0, 0, 0)
            for t in range(TILES):
                stream_evacuate(t)

            def exponentiate(h):
                act.wait_ge(shifted, h + 1)
                nc.scalar.activation(prob[:], prob[:], ACT.Exp).then_inc(exp_ok, 1)

            def head_step(h, r, s, first=False, last=False):
                if not first:
                    exponentiate(h - 1)
                    act.wait_ge(o_ps, h)
                split_out(h, s)
                act.wait_ge(q_ps, h + 1)
                nc.scalar.copy(q_t[:], bank[0][:, 0:ROWS]).then_inc(q_ok, 1)
                if not last:
                    if not first:
                        act.wait_ge(v_ps, h)
                    split_qkv(h + 1, r if s == 0 else r + 1, 1 - s)
                act.wait_ge(k_ps, h + 1)
                nc.scalar.copy(k_t[:], bank[1][:, 0:ROWS]).then_inc(k_ok, 1)
                if not first:
                    act.wait_ge(pt_ps, h)
                    nc.scalar.copy(prob_t[:].rearrange("p t r -> p (t r)"),
                                   bank[3][0:TR, 0:ROWS]).then_inc(pt_ok, 1)
                act.wait_ge(v_ps, h + 1)
                nc.scalar.copy(v_t[:], bank[0][:, 0:ROWS]).then_inc(vt_ok, 1)
                if not first:
                    act.wait_ge(z_ps, h)
                    hi_part(z_hi[:].rearrange("p t r -> p (t r)"),
                            bank[2][:, 0:ROWS]).then_inc(z_hi_ok, 1)
                act.wait_ge(vn_ps, h + 1)
                nc.scalar.copy(v_nat[:].rearrange("p t e -> p (t e)"), bank[3][0:TR, :]).then_inc(vn_ok, 1)

            head_step(0, 0, 0, first=True)
            loop_heads(act, head_step)
            head_step(HEADS - 1, None, 1, last=True)
            exponentiate(HEADS - 1)
            act.wait_ge(pt_ps, HEADS)
            nc.scalar.copy(prob_t[:].rearrange("p t r -> p (t r)"), bank[3][0:TR, 0:ROWS]).then_inc(pt_ok, 1)
            act.wait_ge(z_ps, HEADS)
            hi_part(z_hi[:].rearrange("p t r -> p (t r)"), bank[2][:, 0:ROWS]).then_inc(z_hi_ok, 1)

            for t in range(TILES):
                act.wait_ge(xqt_ps, t + 1)
                hi_part(xq_t[:, t, :], bank[(t + 2) % 4][:, 0:KD * TR]).then_inc(xqt_ok, 1)

        @block.vector
        def _(dve):
            steps = [0]

            def link(ins):
                steps[0] += 1
                ins.then_inc(dve_step, 1)
                dve.wait_ge(dve_step, steps[0])

            def lo_part(dst, src, hi):
                return nc.vector.tensor_tensor(dst, src, hi.bitcast(F32), ALU.subtract)

            def moments_of(t, parts):
                for i, p in enumerate(parts):
                    last = nc.vector.bn_stats(stats[:, t, i, :], p)
                link(last)
                link(nc.vector.bn_aggr(moments[:, t, :], stats[:, t, 0:len(parts), :]))

            def rsqrt_of_variance(lo, hi, eps):
                c = slice(lo, hi)
                v, y = veps[:, c], rstd[:, c]
                n0, n1 = newton[:, 0, c], newton[:, 1, c]
                link(nc.vector.tensor_scalar(v, moments[:, c, 1], eps, None, ALU.add))
                link(nc.vector.tensor_scalar(y.bitcast(I32), v.bitcast(I32), -0.5, RSQRT_SEED,
                                             ALU.mult, ALU.add))
                for _ in range(NEWTON_STEPS):
                    link(nc.vector.scalar_tensor_tensor(out=n0, in0=y, scalar=-0.5, in1=y,
                                                        op0=ALU.mult, op1=ALU.mult))
                    link(nc.vector.tensor_tensor(n1, n0, v, ALU.mult))
                    link(nc.vector.scalar_tensor_tensor(out=y, in0=n1, scalar=1.5, in1=y,
                                                        op0=ALU.add, op1=ALU.mult))

            def patch_scales(t):
                dve.wait_ge(x_landed[t], 16)
                moments_of(t, [x_in[:, t, i * 512:(i + 1) * 512] for i in range(IN_DIM // 512)])
                rsqrt_of_variance(t, t + 1, LN_EPS)
                nc.vector.scalar_tensor_tensor(out=nmr[:, t:t + 1], in0=moments[:, t, 0:1], scalar=-1.0,
                                               in1=rstd[:, t:t + 1], op0=ALU.mult,
                                               op1=ALU.mult).then_inc(x_scaled, 1)

            def patch_evacuate(t):
                dve.wait_ge(xt_ps, t + 1)
                if t >= 2:
                    dve.wait_ge(xt_hi_ok, t - 1)
                    dve.wait_ge(xt_lo_ok, t - 1)
                for k in range(KIN // 2, KIN):
                    last = nc.vector.tensor_scalar(xt[:, t % 2, k * TR:(k + 1) * TR],
                                                   bank[2 * (t % 2) + 1][:, (k - 4) * TR:(k - 3) * TR],
                                                   g1_col[:, k:k + 1], b1_col[:, k:k + 1], ALU.mult, ALU.add)
                last.then_inc(xt_evac_v, 1)
                dve.wait_ge(xt_hi_ok, t + 1)
                if t >= 2:
                    dve.wait_ge(tok_ps, t - 1)
                lo_part(xt_lo[:, t % 2, :], xt[:, t % 2, :], xt_hi[:, t % 2, :]).then_inc(xt_lo_ok, 1)

            def embed_finish(t):
                dve.wait_ge(tok_ps, t + 1)
                h = h_sb[:, t, :]
                link(nc.vector.tensor_tensor(h, acc[t][0:TR, :], tok_b_row[:], ALU.add))
                moments_of(t, [h])
                rsqrt_of_variance(t, t + 1, LN_EPS)
                link(nc.vector.tensor_scalar(h, h, moments[:, t, 0:1], rstd[:, t:t + 1],
                                             ALU.subtract, ALU.mult))
                link(nc.vector.tensor_tensor(h, h, g2_row[:], ALU.mult))
                nc.vector.tensor_tensor(h, h, b2_row[:], ALU.add).then_inc(h_ok, 1)
                dve.wait_ge(h_ok, t + 1)
                moments_of(t, [h])
                rsqrt_of_variance(t, t + 1, NORM_EPS)
                nc.vector.tensor_scalar(hn_sb[:, t, :], h, moments[:, t, 0:1], rstd[:, t:t + 1],
                                        ALU.subtract, ALU.mult).then_inc(hn_ok, 1)

            nc.vector.memset(ones_row[:], 1.0).then_inc(ones_ok, 1)
            patch_scales(0)
            dve.wait_ge(const_in, 16 * N_CONST)
            patch_scales(1)
            for k in range(KIN):
                dve.wait_ge(tokw_hi_ok, k + 1)
                lo_part(tokw_lo[:, k, :], tokw_raw[:, k, :], tokw_hi[:, k, :]).then_inc(tokw_lo_ok, 1)
                if k == 1:
                    patch_evacuate(0)
            patch_evacuate(1)
            for t in range(2, TILES):
                patch_scales(t)
                embed_finish(t - 2)
                patch_evacuate(t)

            def split_qkv(h, s):
                dve.wait_ge(qkvw_hi_ok, h + 1)
                lo_part(qkvw_lo[s][:].rearrange("p a k e -> p (a k e)"), raw[:, s, 0:QKV],
                        qkvw_hi[s][:].rearrange("p a k e -> p (a k e)")).then_inc(qkvw_lo_ok, 1)

            def split_out(h, s):
                dve.wait_ge(outw_hi_ok, h + 1)
                lo_part(outw_lo[s][:], raw[:, s, QKV:WCOLS], outw_hi[s][:]).then_inc(outw_lo_ok, 1)

            embed_finish(TILES - 2)
            split_qkv(0, 0)
            embed_finish(TILES - 1)
            for t in range(TILES):
                dve.wait_ge(ht_hi_ok, t + 1)
                c = slice(t * TR, (t + 1) * TR)
                lo_part(ht_lo[:, :, c], bank[t][:, 0:KD * TR].rearrange("p (k r) -> p k r", k=KD),
                        ht_hi[:, :, c]).then_inc(ht_lo_ok, 1)

            flat = prob[:].rearrange("p t r -> p (t r)")

            def over_keys(col):
                return col[:, :, None].to_broadcast([TR, TILES, TR])

            def softmax_shift(h):
                dve.wait_ge(s_ps, h + 1)
                nc.vector.scalar_tensor_tensor(out=flat, in0=bank[1][0:TR, 0:ROWS], scalar=SCALE,
                                               in1=mask_sb[:], op0=ALU.mult, op1=ALU.add).then_inc(s_read, 1)
                dve.wait_ge(s_read, h + 1)
                nc.vector.tensor_reduce(smax[:], prob[:], AX.X, ALU.max).then_inc(softmax_step, 1)
                dve.wait_ge(softmax_step, h * 3 + 1)
                nc.vector.tensor_tensor(prob[:], prob[:], over_keys(smax), ALU.subtract).then_inc(shifted, 1)

            def softmax_scale(h):
                dve.wait_ge(exp_ok, h + 1)
                nc.vector.tensor_reduce(ssum[:], prob[:], AX.X, ALU.add).then_inc(softmax_step, 1)
                dve.wait_ge(softmax_step, h * 3 + 2)
                nc.vector.reciprocal(srec[:], ssum[:]).then_inc(softmax_step, 1)
                dve.wait_ge(softmax_step, h * 3 + 3)
                nc.vector.tensor_tensor(prob[:], prob[:], over_keys(srec), ALU.mult).then_inc(prob_ok, 1)

            def values_lo(h):
                dve.wait_ge(z_hi_ok, h + 1)
                lo_part(z_lo[:].rearrange("p t r -> p (t r)"), bank[2][:, 0:ROWS],
                        z_hi[:].rearrange("p t r -> p (t r)")).then_inc(z_lo_ok, 1)

            def head_step(h, r, s, first=False, last=False):
                if not first:
                    softmax_shift(h - 1)
                split_out(h, s)
                if not first:
                    softmax_scale(h - 1)
                if not last:
                    split_qkv(h + 1, 1 - s)
                if not first:
                    values_lo(h - 1)

            head_step(0, 0, 0, first=True)
            loop_heads(dve, head_step)
            head_step(HEADS - 1, None, 1, last=True)
            softmax_shift(HEADS - 1)
            dve.wait_ge(ffnw_landed, 16)
            fr, fh, fl = (w.rearrange("p k n -> p (k n)") for w in (ffnw_raw, ffnw_hi, ffnw_lo))
            softmax_scale(HEADS - 1)
            link(nc.vector.tensor_scalar(fr, fr, ffn_scale_col[:], None, ALU.mult))
            values_lo(HEADS - 1)
            nc.vector.tensor_copy(fh, fr).then_inc(ffnw_hi_ok, 1)
            dve.wait_ge(ffnw_hi_ok, 1)
            lo_part(fl, fr, fh).then_inc(ffnw_lo_ok, 1)

            for t in range(TILES):
                dve.wait_ge(o_ps, HEADS + t + 1)
                link(nc.vector.tensor_copy(h_sb[:, t, :], acc[t][0:TR, :]))
                moments_of(t, [h_sb[:, t, :]])
            rsqrt_of_variance(0, TILES, NORM_EPS)
            for t in range(TILES):
                link(nc.vector.tensor_scalar(hn_sb[:, t, :], h_sb[:, t, :], moments[:, t, 0:1],
                                             rstd[:, t:t + 1], ALU.subtract, ALU.mult))
                link(nc.vector.tensor_reduce(tile_max[:, t:t + 1], hn_sb[:, t, :], AX.X, ALU.max,
                                             apply_absolute_value=True))
            nc.vector.tensor_reduce(row_max[:], tile_max[:], AX.X, ALU.max).then_inc(max_ok, 1)
            for t in range(TILES):
                link(nc.vector.tensor_tensor(h_sb[:, t, :], h_sb[:, t, :], ffn_b_row[:], ALU.add))
            dve.wait_ge(max_ps, 1)
            link(nc.vector.tensor_reduce(q_scale[:, 0:1], bank[0][0:1, 0:TR], AX.X, ALU.max))
            link(nc.vector.tensor_scalar(q_scale[:, 0:1], q_scale[:, 0:1], 1.0 / FP8_MAX, SCALE_EPS,
                                         ALU.mult, ALU.max))
            nc.vector.reciprocal(q_scale[:, 1:2], q_scale[:, 0:1]).then_inc(scale_ok, 1)
            dve.wait_ge(scale_ps, 1)
            link(nc.vector.tensor_copy(inv_scale[:], bank[1][0:TR, 0:1]))

            def quantise(t):
                v, m = hn_sb[:, t, :], xq_bits[:, t, :]
                link(nc.vector.tensor_scalar(v, v, inv_scale[:], None, ALU.mult))
                link(nc.vector.tensor_scalar(m.bitcast(I32), v.bitcast(I32), EXP_MASK, None,
                                             ALU.bitwise_and))
                link(nc.vector.tensor_scalar(m, m, FP8_MIN_NORMAL, ROUND_TO_4_BITS, ALU.max, ALU.mult))
                link(nc.vector.tensor_tensor(v, v, m, ALU.add))
                nc.vector.tensor_tensor(v, v, m, ALU.subtract).then_inc(xq_ok, 1)

            def finish(t):
                dve.wait_ge(y_ps, t + 1)
                nc.vector.tensor_tensor(y_sb[:, t, :], acc[t][0:TR, :], h_sb[:, t, :],
                                        ALU.add).then_inc(y_ok, 1)

            for t in range(TILES):
                quantise(t)
                if t >= 2:
                    finish(t - 2)
            for t in range(TILES - 2, TILES):
                finish(t)


def kernel(**inputs):
    import numpy as _np
    import concourse.bacc as _bacc
    from concourse import mybir as _mybir
    from concourse.bass_utils import run_bass_kernel_spmd as _run

    a = {k: _np.asarray(v) for k, v in inputs.items()}
    c = _np.ascontiguousarray
    x = a["x"]

    def chunked(w):
        return w.reshape(w.shape[0] // 128, 128, w.shape[1]).transpose(1, 0, 2)

    def head_in(w):
        return w.reshape(HEADS, E, KD, 128).transpose(0, 3, 2, 1).reshape(HEADS, 128, KD * E)

    heads = _np.concatenate([head_in(a["L0_attn_W_Q"]), head_in(a["L0_attn_W_K"]),
                             head_in(a["L0_attn_W_V"]), a["L0_attn_W_O"].transpose(0, 2, 1)], axis=2)
    r = _np.arange(TR)
    own = (r[:, None] // PATCHES) == (r[None, :] // PATCHES)
    later = r[None, :] > r[:, None]
    mask = _np.where(own, _np.where(later, -1e9, 0.0), -1e30).astype(_np.float32)
    arrays = {
        "patches": c(x[:, :PATCHES * 16, :]).reshape(TILES, TR, IN_DIM),
        "tok_w": c(chunked(a["L0_tok_W"])),
        "heads_w": c(heads),
        "ffn_w": c(chunked(a["L0_ffn_weight"].T)),
        "tok_g1": c(a["L0_tok_g1"].reshape(KIN, 128).T),
        "tok_b1": c(a["L0_tok_b1"].reshape(KIN, 128).T),
        "tok_b": a["L0_tok_b"].reshape(1, D),
        "tok_g2": a["L0_tok_g2"].reshape(1, D),
        "tok_b2": a["L0_tok_b2"].reshape(1, D),
        "ffn_scale": a["L0_ffn_weight_scale"].reshape(1, 1),
        "ffn_bias": a["L0_ffn_bias"].reshape(1, D),
        "mask": c(_np.tile(mask, (1, TILES))),
        "ident": _np.eye(128, dtype=_np.float32),
    }
    nc = _bacc.Bacc("TRN2", target_bir_lowering=False, num_devices=1)
    args = [nc.dram_tensor(n, v.shape, _mybir.dt.from_np(v.dtype), kind="ExternalInput").ap()
            for n, v in arrays.items()]
    out = nc.dram_tensor("out", (TILES, TR, D), _mybir.dt.float32, kind="ExternalOutput").ap()
    audio_tower(nc, *args, out)
    res = _run(nc, [arrays], core_ids=[0])
    return res.results[0]["out"].reshape(BATCH, PATCHES, D)
```

```python
import math
from contextlib import ExitStack

import concourse.bass as bass
from concourse import mybir

ALU = mybir.AluOpType
ACT = mybir.ActivationFunctionType
AX = mybir.AxisListType
F32 = mybir.dt.float32
F32R = mybir.dt.float32r
I32 = mybir.dt.int32

BATCH, PATCHES = 64, 7
ROWS = BATCH * PATCHES
IN_DIM = 1024
D = 512
HEADS, E = 16, 128
TILES = 4
WHOLE = 2
TR = ROWS // TILES
KIN = IN_DIM // 128
KD = D // 128
QKV = 3 * KD * E
WCOLS = QKV + D
SCALE = 1.0 / math.sqrt(E)
LN_EPS, NORM_EPS = 1e-6, 1e-5
FP8_MAX, SCALE_EPS = 448.0, 1e-7
EXP_BITS, HALF_BIT = 0x7F800000, 0x00400000
SHIFT_20 = 2.0 ** 20
ROUND_MIN = 1.5 * 2.0 ** (20 - 6)
NEWTON_SCALE = 2.0 ** 26
NEWTON_STEPS = (3.0, 12.0, 768.0)
RSQRT_SEED = float(0x5F3759DF - 2 ** 31)


def audio_tower(nc, patches, tok_w, heads_w, ffn_w, tok_g1, tok_b1, tok_b, tok_g2, tok_b2,
                ffn_scale, ffn_bias, mask, ident, out):
    with ExitStack() as ctx:
        def sb(name, shape, dt=F32):
            return ctx.enter_context(nc.sbuf_tensor(name, shape, dt))

        def sem(name):
            return ctx.enter_context(nc.semaphore(name))

        ident_sb = sb("ident_sb", [128, 128])
        mask_sb = sb("mask_sb", [TR, TILES * TR])
        g1_col = sb("g1_col", [128, KIN])
        b1_col = sb("b1_col", [128, KIN])
        tok_b_row = sb("tok_b_row", [1, D])
        ffn_b_row = sb("ffn_b_row", [1, D])
        g2_row = sb("g2_row", [TR, D])
        b2_row = sb("b2_row", [TR, D])
        ffn_scale_col = sb("ffn_scale_col", [128, 1])

        x_in = sb("x_in", [TR, TILES, IN_DIM])
        tokw_raw = sb("tokw_raw", [128, KIN, D])
        tokw_hi = sb("tokw_hi", [128, KIN, D], F32R)
        tokw_lo = sb("tokw_lo", [128, KIN, D], F32R)
        xt = sb("xt", [128, 2, KIN * TR])
        xt_hi = sb("xt_hi", [128, 2, KIN * TR], F32R)
        xt_lo = sb("xt_lo", [128, 2, KIN * TR], F32R)

        h_sb = sb("h_sb", [TR, TILES, D])
        hn_sb = sb("hn_sb", [TR, TILES, D])
        ht_hi = sb("ht_hi", [128, KD, ROWS], F32R)
        ht_lo = sb("ht_lo", [128, KD, ROWS], F32R)

        raw = sb("raw", [128, 2, WCOLS])
        qkvw_hi = [sb(f"qkvw_hi{s}", [128, 3, KD, E], F32R) for s in range(2)]
        qkvw_lo = [sb(f"qkvw_lo{s}", [128, 3, KD, E], F32R) for s in range(2)]
        outw_hi = [sb(f"outw_hi{s}", [128, D], F32R) for s in range(2)]
        outw_lo = [sb(f"outw_lo{s}", [128, D], F32R) for s in range(2)]

        q_t = sb("q_t", [128, ROWS])
        k_t = sb("k_t", [128, ROWS])
        v_t = sb("v_t", [128, ROWS])
        v_nat = sb("v_nat", [TR, TILES, E])
        prob = sb("prob", [TR, TILES, TR])
        prob_t = sb("prob_t", [TR, TILES, TR])
        z_hi = sb("z_hi", [128, TILES, TR], F32R)
        z_lo = sb("z_lo", [128, TILES, TR], F32R)
        smax = sb("smax", [TR, TILES])
        ssum = sb("ssum", [TR, TILES])
        srec = sb("srec", [TR, TILES])

        ffnw_raw, ffnw_hi, ffnw_lo = tokw_raw[:, 0:KD, :], tokw_hi[:, 0:KD, :], tokw_lo[:, 0:KD, :]
        xq_bits = x_in[:, :, 0:D]
        y_sb = x_in[:, :, D:2 * D]
        xq_t = xt_hi[:].rearrange("p a (b c) -> p (a b) c", b=2)

        NCOL = 4 * TILES
        stats = sb("stats", [TR, NCOL, 2, 6])
        moments = sb("moments", [TR, NCOL, 2])
        vscaled = sb("vscaled", [TR, NCOL])
        newton = sb("newton", [TR, NCOL])
        rstd = sb("rstd", [TR, NCOL])
        nmr = sb("nmr", [TR, NCOL])
        neg_mean = sb("neg_mean", [TR, TILES])
        ones_sb = sb("ones_sb", [TR, TR])
        tile_max = sb("tile_max", [TR, TILES])
        row_max = sb("row_max", [TR, 1])
        max_diag = sb("max_diag", [TR, TR])
        q_scale = sb("q_scale", [TR, 3])
        q_factor = sb("q_factor", [TR, TILES])
        q_factor_20 = sb("q_factor_20", [TR, TILES])

        bank = [ctx.enter_context(nc.psum_tensor(f"bank{i}", [128, 512], F32)) for i in range(4)]
        acc = [ctx.enter_context(nc.psum_tensor(f"acc{t}", [128, D], F32)) for t in range(TILES)]

        ident_landed = sem("ident_landed")
        cols_landed = sem("cols_landed")
        tok_b_landed = sem("tok_b_landed")
        rows_landed = sem("rows_landed")
        late_landed = sem("late_landed")
        x_landed = [sem(f"x_landed{t}") for t in range(TILES)]
        tokw_landed = [sem(f"tokw_landed{i}") for i in range(2)]
        raw_landed = [sem(f"raw_landed{s}") for s in range(2)]
        ffnw_landed = sem("ffnw_landed")
        out_stored = sem("out_stored")

        dve_step = sem("dve_step")
        x_scaled = sem("x_scaled")
        x_normed = sem("x_normed")
        xt_ps = sem("xt_ps")
        xt_ok = sem("xt_ok")
        xt_hi_ok = sem("xt_hi_ok")
        xt_lo_ok = sem("xt_lo_ok")
        tokw_hi_ok = sem("tokw_hi_ok")
        tokw_lo_ok = sem("tokw_lo_ok")
        tok_ps = sem("tok_ps")
        h_ok = sem("h_ok")
        hn_ok = sem("hn_ok")
        ht_ps = sem("ht_ps")
        ht_hi_ok = sem("ht_hi_ok")
        ht_lo_ok = sem("ht_lo_ok")

        qkvw_hi_ok = sem("qkvw_hi_ok")
        qkvw_lo_ok = sem("qkvw_lo_ok")
        outw_hi_ok = sem("outw_hi_ok")
        outw_lo_ok = sem("outw_lo_ok")
        q_ps, k_ps, v_ps = sem("q_ps"), sem("k_ps"), sem("v_ps")
        q_ok, k_ok, vt_ok = sem("q_ok"), sem("k_ok"), sem("vt_ok")
        s_ps = sem("s_ps")
        s_read = sem("s_read")
        shifted = sem("shifted")
        exp_ok = sem("exp_ok")
        prob_ok = sem("prob_ok")
        pt_ps, pt_ok = sem("pt_ps"), sem("pt_ok")
        vn_ps, vn_ok = sem("vn_ps"), sem("vn_ok")
        z_ps, z_hi_ok, z_lo_ok = sem("z_ps"), sem("z_hi_ok"), sem("z_lo_ok")
        o_ps = sem("o_ps")
        softmax_step = sem("softmax_step")

        ffnw_hi_ok = sem("ffnw_hi_ok")
        ffnw_lo_ok = sem("ffnw_lo_ok")
        ones_ok = sem("ones_ok")
        mean_ok = sem("mean_ok")
        magnitude_ok = sem("magnitude_ok")
        centred = sem("centred")
        diag_ok = sem("diag_ok")
        max_ps = sem("max_ps")
        factor_ok = sem("factor_ok")
        bits_ok = sem("bits_ok")
        scaled_ok = sem("scaled_ok")
        xq_ok = sem("xq_ok")
        xqt_ps = sem("xqt_ps")
        xqt_ok = sem("xqt_ok")
        y_ps = sem("y_ps")
        y_even_ok = sem("y_even_ok")
        y_odd_ok = sem("y_odd_ok")

        ht_bank = (bank[0], bank[1], bank[3], acc[3])
        block = ctx.enter_context(nc.Block())

        def loop_heads(eng, step):
            with eng.Fori(0, (HEADS - 2) // 2) as i:
                step(i * 2 + 1, i, 1)
                step(i * 2 + 2, i + 1, 0)

        @block.sync
        def _(sp):
            def load(dst, src, landed):
                sp.dma_start(dst, src).then_inc(landed, 16)

            half = KIN // 2
            load(x_in[:, 0, :], patches[0], x_landed[0])
            load(tokw_raw[:, 0:half, :], tok_w[:, 0:half, :], tokw_landed[0])
            load(ident_sb[:], ident, ident_landed)
            load(g1_col[:], tok_g1, cols_landed)
            load(b1_col[:], tok_b1, cols_landed)
            load(x_in[:, 1, :], patches[1], x_landed[1])
            load(tok_b_row[:], tok_b, tok_b_landed)
            load(tokw_raw[:, half:KIN, :], tok_w[:, half:KIN, :], tokw_landed[1])
            load(x_in[:, 2, :], patches[2], x_landed[2])
            load(x_in[:, 3, :], patches[3], x_landed[3])
            load(g2_row[:], tok_g2.to_broadcast([TR, D]), rows_landed)
            load(b2_row[:], tok_b2.to_broadcast([TR, D]), rows_landed)
            load(mask_sb[:], mask, late_landed)
            load(ffn_scale_col[:], ffn_scale.to_broadcast([128, 1]), late_landed)
            load(ffn_b_row[:], ffn_bias, late_landed)
            for s in range(2):
                sp.dma_start(raw[:, s, :], heads_w[s]).then_inc(raw_landed[s], 16)
            sp.wait_ge(tokw_lo_ok, KIN)
            sp.wait_ge(tok_ps, WHOLE)
            sp.dma_start(ffnw_raw, ffn_w).then_inc(ffnw_landed, 16)

            def load_head(h, _, s):
                sp.wait_ge(outw_hi_ok, h)
                sp.wait_ge(outw_lo_ok, h)
                sp.dma_start(raw[:, 1 - s, :], heads_w[h + 1]).then_inc(raw_landed[1 - s], 16)

            loop_heads(sp, load_head)
            for t in range(TILES):
                sp.wait_ge((y_even_ok, y_odd_ok)[t % 2], t // 2 + 1)
                sp.dma_start(out[t], h_sb[:, t, :]).then_inc(out_stored, 16)
            sp.wait_ge(out_stored, 16 * TILES)

        @block.tensor
        def _(pe):
            def split_product(ps, hi, lo, whi, wlo, first, last):
                nc.tensor.matmul(ps, hi, whi, start=first, stop=False, skip_group_check=True)
                nc.tensor.matmul(ps, hi, wlo, start=False, stop=False, skip_group_check=True)
                return nc.tensor.matmul(ps, lo, whi, start=False, stop=last, skip_group_check=True)

            def patch_transposes(t):
                pe.wait_ge(x_normed, t + 1)
                if t == 0:
                    pe.wait_ge(ident_landed, 16)
                if t >= 2:
                    pe.wait_ge(xt_ok, 2 * (t - 1))
                for k in range(KIN):
                    b = 2 * (t % 2) + k // 4
                    mm = nc.tensor.transpose(bank[b][:, k % 4 * TR:(k % 4 + 1) * TR],
                                             x_in[:, t, k * 128:(k + 1) * 128], ident_sb[0:TR, 0:TR])
                    if k % 4 == 3:
                        mm.then_inc(xt_ps, 1)

            def embed(t, half):
                if half == 0:
                    if t == 0:
                        pe.wait_ge(tok_b_landed, 16)
                        pe.wait_ge(ones_ok, 1)
                    nc.tensor.matmul(acc[t][0:TR, :], ones_sb[0:1, :], tok_b_row[:], start=True, stop=False,
                                     skip_group_check=True)
                pe.wait_ge(xt_ok, 2 * t + half + 1)
                if t == 0:
                    pe.wait_ge(tokw_landed[half], 16)
                elif t >= WHOLE:
                    pe.wait_ge(xt_hi_ok, 2 * (t - WHOLE) + half + 1)
                    pe.wait_ge(xt_lo_ok, 2 * (t - WHOLE) + half + 1)
                    pe.wait_ge(tokw_hi_ok, (half + 1) * KIN // 2)
                    pe.wait_ge(tokw_lo_ok, (half + 1) * KIN // 2)
                for k in range(half * KIN // 2, (half + 1) * KIN // 2):
                    c = slice(k * TR, (k + 1) * TR)
                    if t < WHOLE:
                        last = nc.tensor.matmul(acc[t][0:TR, :], xt[:, t % 2, c], tokw_raw[:, k, :],
                                                start=False, stop=(k == KIN - 1), skip_group_check=True)
                    else:
                        last = split_product(acc[t][0:TR, :], xt_hi[:, t % 2, c], xt_lo[:, t % 2, c],
                                             tokw_hi[:, k, :], tokw_lo[:, k, :], False, k == KIN - 1)
                if half == 1:
                    last.then_inc(tok_ps, 1)

            def stream_transposes(t):
                pe.wait_ge(hn_ok, t + 1)
                if t == 0:
                    pe.wait_ge(xt_ok, 2 * TILES)
                for k in range(KD):
                    last = nc.tensor.transpose(ht_bank[t][:, k * TR:(k + 1) * TR],
                                               hn_sb[:, t, k * 128:(k + 1) * 128], ident_sb[0:TR, 0:TR])
                last.then_inc(ht_ps, 1)

            def seed(t):
                pe.wait_ge(h_ok, t + 1)
                mm = nc.tensor.matmul(acc[t][0:TR, :], ident_sb[0:TR, 0:TR], h_sb[:, t, :],
                                      start=True, stop=False, skip_group_check=True)
                if t == TILES - 1:
                    mm.then_inc(o_ps, 1)

            patch_transposes(0)
            for t in range(TILES):
                embed(t, 0)
                if t + 1 < TILES:
                    patch_transposes(t + 1)
                embed(t, 1)
                if t == TILES - 1:
                    for done in range(2):
                        stream_transposes(done)
                        seed(done)

            def project(which, ps, s, done=None, rows=slice(0, ROWS)):
                for k in range(KD):
                    wh, wl = qkvw_hi[s][:, which, k, :], qkvw_lo[s][:, which, k, :]
                    last = split_product(ps[:, rows], wh, wl, ht_hi[:, k, rows], ht_lo[:, k, rows],
                                         k == 0, k == KD - 1)
                if done is not None:
                    last.then_inc(done, 1)

            def project_q(h, s):
                pe.wait_ge(qkvw_hi_ok, h + 1)
                pe.wait_ge(qkvw_lo_ok, h + 1)
                project(0, bank[0], s, q_ps)

            def project_v(h, s):
                pe.wait_ge(q_ok, h + 1)
                project(2, bank[0], s, v_ps)

            def prob_transposes(h):
                pe.wait_ge(prob_ok, h + 1)
                pe.wait_ge(vn_ok, h + 1)
                for t in range(TILES):
                    last = nc.tensor.transpose(bank[3][0:TR, t * TR:(t + 1) * TR], prob[:, t, :],
                                               ident_sb[0:TR, 0:TR])
                last.then_inc(pt_ps, 1)

            def weigh_values(h):
                pe.wait_ge(pt_ok, h + 1)
                for t in range(TILES):
                    last = nc.tensor.matmul(bank[2][:, t * TR:(t + 1) * TR], v_nat[:, t, :],
                                            prob_t[:, t, :], start=True, stop=True)
                last.then_inc(z_ps, 1)

            def scores(h):
                pe.wait_ge(k_ok, h + 1)
                for t in range(TILES):
                    c = slice(t * TR, (t + 1) * TR)
                    last = nc.tensor.matmul(bank[1][0:TR, c], q_t[:, c], k_t[:, c], start=True, stop=True)
                last.then_inc(s_ps, 1)

            def value_transposes(h):
                pe.wait_ge(vt_ok, h + 1)
                for t in range(TILES):
                    last = nc.tensor.transpose(bank[3][0:TR, t * E:(t + 1) * E],
                                               v_t[:, t * TR:(t + 1) * TR], ident_sb[:])
                last.then_inc(vn_ps, 1)

            def project_out(h, s, final=False):
                pe.wait_ge(outw_hi_ok, h + 1)
                pe.wait_ge(outw_lo_ok, h + 1)
                pe.wait_ge(z_hi_ok, h + 1)
                if not final:
                    for t in range(TILES):
                        for w in (outw_hi[s], outw_lo[s]):
                            nc.tensor.matmul(acc[t][0:TR, :], z_hi[:, t, :], w[:], start=False, stop=False,
                                             skip_group_check=True)
                    pe.wait_ge(z_lo_ok, h + 1)
                    for t in range(TILES):
                        last = nc.tensor.matmul(acc[t][0:TR, :], z_lo[:, t, :], outw_hi[s][:], start=False,
                                                stop=False, skip_group_check=True)
                    last.then_inc(o_ps, 1)
                else:
                    pe.wait_ge(z_lo_ok, h + 1)
                    for t in range(TILES):
                        split_product(acc[t][0:TR, :], z_hi[:, t, :], z_lo[:, t, :], outw_hi[s][:],
                                      outw_lo[s][:], False, True).then_inc(o_ps, 1)

            def head_step(h, _, s):
                project_q(h, s)
                pe.wait_ge(s_read, h)
                project(1, bank[1], s, k_ps)
                prob_transposes(h - 1)
                project_v(h, s)
                weigh_values(h - 1)
                scores(h)
                value_transposes(h)
                project_out(h - 1, 1 - s)

            pe.wait_ge(qkvw_hi_ok, 1)
            pe.wait_ge(qkvw_lo_ok, 1)
            pe.wait_ge(ht_hi_ok, 2)
            pe.wait_ge(ht_lo_ok, 2)
            first_half, second_half = slice(0, ROWS // 2), slice(ROWS // 2, ROWS)
            project(0, bank[0], 0, rows=first_half)
            project(1, bank[1], 0, rows=first_half)
            stream_transposes(2)
            seed(2)
            project(2, bank[2], 0, rows=first_half)
            stream_transposes(3)
            pe.wait_ge(ht_hi_ok, TILES)
            pe.wait_ge(ht_lo_ok, TILES)
            for which, done in enumerate((q_ps, k_ps, v_ps)):
                project(which, bank[which], 0, done, rows=second_half)
            seed(3)
            pe.wait_ge(q_ok, 1)
            scores(0)
            value_transposes(0)

            loop_heads(pe, head_step)

            h, s = HEADS - 1, (HEADS - 1) % 2
            project_q(h, s)
            pe.wait_ge(s_read, h)
            project(1, bank[1], s, k_ps)
            prob_transposes(h - 1)
            pe.wait_ge(q_ok, h + 1)
            scores(h)
            project_v(h, s)
            weigh_values(h - 1)
            value_transposes(h)
            project_out(h - 1, 1 - s)
            prob_transposes(h)
            weigh_values(h)
            project_out(h, s, final=True)

            pe.wait_ge(diag_ok, 1)
            nc.tensor.matmul(bank[1][0:TR, 0:TR], ones_sb[:], max_diag[:], start=True,
                             stop=True).then_inc(max_ps, 1)
            pe.wait_ge(late_landed, 48)
            pe.wait_ge(centred, TILES)
            for t in range(TILES):
                nc.tensor.matmul(acc[t][0:TR, :], ones_sb[0:1, :], ffn_b_row[:], start=False, stop=False,
                                 skip_group_check=True)
            pe.wait_ge(ffnw_hi_ok, 1)
            pe.wait_ge(ffnw_lo_ok, 1)

            def quantised_transposes(t):
                pe.wait_ge(xq_ok, t + 1)
                if t == 3:
                    pe.wait_ge(factor_ok, 1)
                for k in range(KD):
                    last = nc.tensor.transpose(bank[(t + 2) % 4][:, k * TR:(k + 1) * TR],
                                               hn_sb[:, t, k * 128:(k + 1) * 128], ident_sb[0:TR, 0:TR])
                last.then_inc(xqt_ps, 1)

            def feed_forward(t):
                pe.wait_ge(xqt_ok, t + 1)
                for k in range(KD):
                    for w in (ffnw_hi, ffnw_lo):
                        last = nc.tensor.matmul(acc[t][0:TR, :], xq_t[:, t, k * TR:(k + 1) * TR], w[:, k, :],
                                                start=False, stop=(k == KD - 1 and w is ffnw_lo),
                                                skip_group_check=True)
                last.then_inc(y_ps, 1)

            for t in range(TILES):
                quantised_transposes(t)
                if t >= 1:
                    feed_forward(t - 1)
            feed_forward(TILES - 1)

        @block.scalar
        def _(act):
            def hi_part(dst, src):
                return nc.scalar.copy(dst, src)

            def normalise(t):
                act.wait_ge(x_scaled, t + 1)
                nc.scalar.activation(x_in[:, t, :], x_in[:, t, :], ACT.Identity, bias=nmr[:, t:t + 1],
                                     scale=rstd[:, t:t + 1]).then_inc(x_normed, 1)

            def patch_evacuate(t):
                for half in range(2):
                    act.wait_ge(xt_ps, 2 * t + half + 1)
                    if t >= 2 and half == 0:
                        act.wait_ge(tok_ps, t - 1)
                    for k in range(half * KIN // 2, (half + 1) * KIN // 2):
                        last = nc.scalar.activation(xt[:, t % 2, k * TR:(k + 1) * TR],
                                                    bank[2 * (t % 2) + half][:, k % 4 * TR:(k % 4 + 1) * TR],
                                                    ACT.Identity, bias=b1_col[:, k:k + 1],
                                                    scale=g1_col[:, k:k + 1])
                    last.then_inc(xt_ok, 1)
                    if t >= WHOLE:
                        act.wait_ge(xt_ok, 2 * t + half + 1)
                        c = slice(half * KIN // 2 * TR, (half + 1) * KIN // 2 * TR)
                        hi_part(xt_hi[:, t % 2, c], xt[:, t % 2, c]).then_inc(xt_hi_ok, 1)

            def stream_evacuate(t):
                act.wait_ge(ht_ps, t + 1)
                hi_part(ht_hi[:, :, t * TR:(t + 1) * TR],
                        ht_bank[t][:, 0:KD * TR].rearrange("p (k r) -> p k r", k=KD)).then_inc(ht_hi_ok, 1)

            def embed_weights(half):
                act.wait_ge(tokw_landed[half], 16)
                for k in range(half * KIN // 2, (half + 1) * KIN // 2):
                    hi_part(tokw_hi[:, k, :], tokw_raw[:, k, :]).then_inc(tokw_hi_ok, 1)

            def split_qkv(h, r, s):
                act.wait_ge(raw_landed[s], (r + 1) * 16)
                hi_part(qkvw_hi[s][:].rearrange("p a k e -> p (a k e)"),
                        raw[:, s, 0:QKV]).then_inc(qkvw_hi_ok, 1)

            def split_out(h, s):
                hi_part(outw_hi[s][:], raw[:, s, QKV:WCOLS]).then_inc(outw_hi_ok, 1)

            normalise(0)
            act.wait_ge(cols_landed, 32)
            patch_evacuate(0)
            normalise(1)
            embed_weights(0)
            patch_evacuate(1)
            normalise(2)
            embed_weights(1)
            normalise(3)
            patch_evacuate(2)
            split_qkv(0, 0, 0)
            patch_evacuate(3)
            for t in range(2):
                stream_evacuate(t)
            split_qkv(1, 0, 1)
            split_out(0, 0)
            for t in range(2, TILES):
                stream_evacuate(t)

            def exponentiate(h):
                act.wait_ge(shifted, h + 1)
                nc.scalar.activation(prob[:], prob[:], ACT.Exp).then_inc(exp_ok, 1)

            def copy_probs(h):
                act.wait_ge(pt_ps, h + 1)
                nc.scalar.copy(prob_t[:].rearrange("p t r -> p (t r)"),
                               bank[3][0:TR, 0:ROWS]).then_inc(pt_ok, 1)

            def copy_q(h):
                act.wait_ge(q_ps, h + 1)
                nc.scalar.copy(q_t[:], bank[0][:, 0:ROWS]).then_inc(q_ok, 1)

            def copy_k(h):
                act.wait_ge(k_ps, h + 1)
                nc.scalar.copy(k_t[:], bank[1][:, 0:ROWS]).then_inc(k_ok, 1)

            def copy_v(h, b=0):
                act.wait_ge(v_ps, h + 1)
                nc.scalar.copy(v_t[:], bank[b][:, 0:ROWS]).then_inc(vt_ok, 1)

            def copy_v_rows(h):
                act.wait_ge(vn_ps, h + 1)
                nc.scalar.copy(v_nat[:].rearrange("p t e -> p (t e)"), bank[3][0:TR, :]).then_inc(vn_ok, 1)

            def values_hi(h):
                act.wait_ge(z_ps, h + 1)
                hi_part(z_hi[:].rearrange("p t r -> p (t r)"), bank[2][:, 0:ROWS]).then_inc(z_hi_ok, 1)

            def head_step(h, r, s):
                exponentiate(h - 1)
                act.wait_ge(o_ps, h)
                split_out(h, s)
                copy_q(h)
                act.wait_ge(v_ps, h)
                split_qkv(h + 1, r if s == 0 else r + 1, 1 - s)
                copy_k(h)
                copy_probs(h - 1)
                copy_v(h)
                values_hi(h - 1)
                copy_v_rows(h)

            copy_q(0)
            copy_k(0)
            copy_v(0, 2)
            copy_v_rows(0)

            loop_heads(act, head_step)

            h, s = HEADS - 1, (HEADS - 1) % 2
            exponentiate(h - 1)
            act.wait_ge(o_ps, h)
            split_out(h, s)
            copy_q(h)
            copy_k(h)
            copy_probs(h - 1)
            copy_v(h)
            exponentiate(h)
            values_hi(h - 1)
            copy_v_rows(h)
            copy_probs(h)
            values_hi(h)

            for t in range(TILES):
                act.wait_ge(mean_ok, t + 1)
                nc.scalar.activation(hn_sb[:, t, :], acc[t][0:TR, :], ACT.Identity,
                                     bias=neg_mean[:, t:t + 1]).then_inc(centred, 1)

            def magnitudes(t):
                nc.scalar.mul(xq_bits[:, t, :], hn_sb[:, t, :], q_factor_20[:, t:t + 1]).then_inc(bits_ok, 1)

            act.wait_ge(factor_ok, 2)
            act.wait_ge(centred, TILES)
            magnitudes(0)
            for t in range(1, TILES):
                magnitudes(t)
                nc.scalar.mul(y_sb[:, t, :], hn_sb[:, t, :], q_factor[:, t:t + 1]).then_inc(scaled_ok, 1)
                act.wait_ge(xqt_ps, t)
                hi_part(xq_t[:, t - 1, :], bank[(t + 1) % 4][:, 0:KD * TR]).then_inc(xqt_ok, 1)
            act.wait_ge(xqt_ps, TILES)
            hi_part(xq_t[:, TILES - 1, :], bank[(TILES + 1) % 4][:, 0:KD * TR]).then_inc(xqt_ok, 1)
            for t in range(0, TILES, 2):
                act.wait_ge(y_ps, t + 1)
                nc.scalar.copy(h_sb[:, t, :], acc[t][0:TR, :]).then_inc(y_even_ok, 1)

        @block.vector
        def _(dve):
            steps = [0]

            def mark(ins):
                steps[0] += 1
                ins.then_inc(dve_step, 1)
                return steps[0]

            def need(step):
                dve.wait_ge(dve_step, step)

            def link(ins):
                need(mark(ins))

            def lo_part(dst, src, hi):
                return nc.vector.tensor_tensor(dst, src, hi.bitcast(F32), ALU.subtract)

            def moments_of(c, parts):
                for i, p in enumerate(parts):
                    last = nc.vector.bn_stats(stats[:, c, i, :], p)
                link(last)
                return mark(nc.vector.bn_aggr(moments[:, c, :], stats[:, c, 0:len(parts), :]))

            def rsqrt(columns, moments_step, between=None):
                done = {c: moments_step for c, _ in columns}
                for i in range(2 + 2 * len(NEWTON_STEPS)):
                    for c, eps in columns:
                        v, y, n = vscaled[:, c:c + 1], rstd[:, c:c + 1], newton[:, c:c + 1]
                        need(done[c])
                        if i == 0:
                            ins = nc.vector.tensor_scalar(v, moments[:, c, 1:2], eps, NEWTON_SCALE,
                                                          ALU.add, ALU.mult)
                        elif i == 1:
                            ins = nc.vector.tensor_scalar(y.bitcast(I32), v.bitcast(I32), -0.5, RSQRT_SEED,
                                                          ALU.mult, ALU.add)
                        elif i % 2 == 0:
                            ins = nc.vector.tensor_scalar(n, y, y, v, ALU.mult, ALU.mult)
                        else:
                            ins = nc.vector.scalar_tensor_tensor(out=y, in0=n, scalar=NEWTON_STEPS[i // 2 - 1],
                                                                 in1=y, op0=ALU.subtract, op1=ALU.mult)
                        done[c] = mark(ins)
                    if between is not None:
                        between(i)
                return max(done.values())

            def negative_mean_scaled(c):
                return nc.vector.scalar_tensor_tensor(out=nmr[:, c:c + 1], in0=moments[:, c, 0:1],
                                                      scalar=-1.0, in1=rstd[:, c:c + 1],
                                                      op0=ALU.mult, op1=ALU.mult)

            def patch_moments(t):
                dve.wait_ge(x_landed[t], 16)
                return moments_of(t, [x_in[:, t, i * 512:(i + 1) * 512] for i in range(IN_DIM // 512)])

            def patch_lo(t, half):
                dve.wait_ge(xt_hi_ok, 2 * (t - WHOLE) + half + 1)
                c = slice(half * KIN // 2 * TR, (half + 1) * KIN // 2 * TR)
                lo_part(xt_lo[:, t % 2, c], xt[:, t % 2, c], xt_hi[:, t % 2, c]).then_inc(xt_lo_ok, 1)

            def embed_weights_lo(k):
                dve.wait_ge(tokw_hi_ok, k + 1)
                lo_part(tokw_lo[:, k, :], tokw_raw[:, k, :], tokw_hi[:, k, :]).then_inc(tokw_lo_ok, 1)

            def stream_lo(t):
                dve.wait_ge(ht_hi_ok, t + 1)
                c = slice(t * TR, (t + 1) * TR)
                lo_part(ht_lo[:, :, c], ht_bank[t][:, 0:KD * TR].rearrange("p (k r) -> p k r", k=KD),
                        ht_hi[:, :, c]).then_inc(ht_lo_ok, 1)

            stream_step = {}

            def stream_norms(t, between=None):
                columns = []
                if t < TILES:
                    c = TILES + t
                    dve.wait_ge(tok_ps, t + 1)
                    step = moments_of(c, [acc[t][0:TR, :]])
                    need(step)
                    centred_step = mark(nc.vector.scalar_tensor_tensor(
                        out=h_sb[:, t, :], in0=acc[t][0:TR, :], scalar=moments[:, c, 0:1], in1=g2_row[:],
                        op0=ALU.subtract, op1=ALU.mult))
                    columns.append((c, LN_EPS))
                else:
                    step = stream_step[t - 1]
                if t >= 1:
                    columns.append((2 * TILES + t - 1, NORM_EPS))
                need(rsqrt(columns, step, between))
                if t < TILES:
                    need(centred_step)
                    nc.vector.scalar_tensor_tensor(out=h_sb[:, t, :], in0=h_sb[:, t, :],
                                                   scalar=rstd[:, c:c + 1], in1=b2_row[:],
                                                   op0=ALU.mult, op1=ALU.add).then_inc(h_ok, 1)
                if t >= 1:
                    p = 2 * TILES + t - 1
                    nc.vector.tensor_scalar(hn_sb[:, t - 1, :], h_sb[:, t - 1, :], moments[:, p, 0:1],
                                            rstd[:, p:p + 1], ALU.subtract, ALU.mult).then_inc(hn_ok, 1)
                if t < TILES:
                    dve.wait_ge(h_ok, t + 1)
                    stream_step[t] = moments_of(2 * TILES + t, [h_sb[:, t, :]])

            def split_qkv(h, s):
                dve.wait_ge(qkvw_hi_ok, h + 1)
                lo_part(qkvw_lo[s][:].rearrange("p a k e -> p (a k e)"), raw[:, s, 0:QKV],
                        qkvw_hi[s][:].rearrange("p a k e -> p (a k e)")).then_inc(qkvw_lo_ok, 1)

            def split_out(h, s):
                dve.wait_ge(outw_hi_ok, h + 1)
                lo_part(outw_lo[s][:], raw[:, s, QKV:WCOLS], outw_hi[s][:]).then_inc(outw_lo_ok, 1)

            nc.vector.memset(ones_sb[:], 1.0).then_inc(ones_ok, 1)
            need(rsqrt([(0, LN_EPS)], patch_moments(0)))
            negative_mean_scaled(0).then_inc(x_scaled, 1)
            need(rsqrt([(1, LN_EPS)], patch_moments(1)))
            negative_mean_scaled(1).then_inc(x_scaled, 1)
            patch_moments(2)
            need(rsqrt([(2, LN_EPS), (3, LN_EPS)], patch_moments(3),
                       between=lambda i: embed_weights_lo(i // 2) if i % 2 else None))
            negative_mean_scaled(2).then_inc(x_scaled, 1)
            negative_mean_scaled(3).then_inc(x_scaled, 1)
            dve.wait_ge(rows_landed, 32)
            for k in range(KIN // 2, KIN):
                embed_weights_lo(k)
            stream_norms(0)
            patch_lo(2, 0)
            patch_lo(2, 1)
            stream_norms(1, between=lambda i: split_qkv(0, 0) if i == 4 else None)
            patch_lo(3, 0)
            patch_lo(3, 1)
            stream_norms(2)
            stream_norms(3, between=lambda i: stream_lo((i - 2) // 2) if i in (2, 4) else None)
            stream_norms(TILES)
            stream_lo(2)
            stream_lo(3)

            flat = prob[:].rearrange("p t r -> p (t r)")

            def over_keys(col):
                return col[:, :, None].to_broadcast([TR, TILES, TR])

            def softmax_shift(h):
                dve.wait_ge(s_ps, h + 1)
                nc.vector.scalar_tensor_tensor(out=flat, in0=bank[1][0:TR, 0:ROWS], scalar=SCALE,
                                               in1=mask_sb[:], op0=ALU.mult, op1=ALU.add).then_inc(s_read, 1)
                dve.wait_ge(s_read, h + 1)
                nc.vector.tensor_reduce(smax[:], prob[:], AX.X, ALU.max).then_inc(softmax_step, 1)
                dve.wait_ge(softmax_step, h * 3 + 1)
                nc.vector.tensor_tensor(prob[:], prob[:], over_keys(smax), ALU.subtract).then_inc(shifted, 1)

            def softmax_scale(h):
                dve.wait_ge(exp_ok, h + 1)
                nc.vector.tensor_reduce(ssum[:], prob[:], AX.X, ALU.add).then_inc(softmax_step, 1)
                dve.wait_ge(softmax_step, h * 3 + 2)
                nc.vector.reciprocal(srec[:], ssum[:]).then_inc(softmax_step, 1)
                dve.wait_ge(softmax_step, h * 3 + 3)
                nc.vector.tensor_tensor(prob[:], prob[:], over_keys(srec), ALU.mult).then_inc(prob_ok, 1)

            def values_lo(h):
                dve.wait_ge(z_hi_ok, h + 1)
                lo_part(z_lo[:].rearrange("p t r -> p (t r)"), bank[2][:, 0:ROWS],
                        z_hi[:].rearrange("p t r -> p (t r)")).then_inc(z_lo_ok, 1)

            def head_step(h, r, s):
                softmax_shift(h - 1)
                split_out(h, s)
                softmax_scale(h - 1)
                split_qkv(h + 1, 1 - s)
                values_lo(h - 1)

            split_qkv(1, 1)
            split_out(0, 0)
            dve.wait_ge(ffnw_landed, 16)
            dve.wait_ge(late_landed, 48)
            fr, fh, fl = (w.rearrange("p k n -> p (k n)") for w in (ffnw_raw, ffnw_hi, ffnw_lo))
            link(nc.vector.tensor_scalar(fr, fr, ffn_scale_col[:], None, ALU.mult))
            nc.vector.tensor_copy(fh, fr).then_inc(ffnw_hi_ok, 1)
            dve.wait_ge(ffnw_hi_ok, 1)
            lo_part(fl, fr, fh).then_inc(ffnw_lo_ok, 1)

            loop_heads(dve, head_step)

            h, s = HEADS - 1, (HEADS - 1) % 2
            softmax_shift(h - 1)
            split_out(h, s)
            softmax_scale(h - 1)
            dve.wait_ge(pt_ps, h)
            softmax_shift(h)
            values_lo(h - 1)
            softmax_scale(h)
            values_lo(h)

            last_col = 3 * TILES

            def magnitude(t):
                dve.wait_ge(centred, t + 1)
                nc.vector.tensor_reduce(tile_max[:, t:t + 1], hn_sb[:, t, :], AX.X, ALU.max,
                                        apply_absolute_value=True).then_inc(magnitude_ok, 1)

            for t in range(TILES):
                dve.wait_ge(o_ps, HEADS + t + 1)
                need(moments_of(last_col + t, [acc[t][0:TR, :]]))
                nc.vector.tensor_scalar(neg_mean[:, t:t + 1], moments[:, last_col + t, 0:1], -1.0, None,
                                        ALU.mult).then_inc(mean_ok, 1)
            c = slice(last_col, last_col + TILES)
            v, rs, n = vscaled[:, c], rstd[:, c], newton[:, c]
            link(nc.vector.tensor_scalar(v, moments[:, c, 1], NORM_EPS, NEWTON_SCALE, ALU.add, ALU.mult))
            link(nc.vector.tensor_scalar(rs.bitcast(I32), v.bitcast(I32), -0.5, RSQRT_SEED,
                                         ALU.mult, ALU.add))
            for i, step in enumerate(NEWTON_STEPS):
                square = mark(nc.vector.tensor_tensor(n, rs, rs, ALU.mult))
                magnitude(i)
                need(square)
                link(nc.vector.tensor_tensor(n, n, v, ALU.mult))
                link(nc.vector.scalar_tensor_tensor(out=rs, in0=n, scalar=step, in1=rs,
                                                    op0=ALU.subtract, op1=ALU.mult))
            magnitude(TILES - 1)
            dve.wait_ge(magnitude_ok, TILES)
            link(nc.vector.tensor_tensor(tile_max[:], tile_max[:], rs, ALU.mult))
            link(nc.vector.tensor_reduce(row_max[:], tile_max[:], AX.X, ALU.max))
            nc.vector.tensor_scalar(max_diag[:], ident_sb[0:TR, 0:TR], row_max[:], None,
                                    ALU.mult).then_inc(diag_ok, 1)
            dve.wait_ge(max_ps, 1)
            link(nc.vector.tensor_reduce(q_scale[:, 0:1], bank[1][0:TR, 0:TR], AX.X, ALU.max))
            link(nc.vector.tensor_scalar(q_scale[:, 1:2], q_scale[:, 0:1], 1.0 / FP8_MAX, SCALE_EPS,
                                         ALU.mult, ALU.max))
            link(nc.vector.reciprocal(q_scale[:, 2:3], q_scale[:, 1:2]))
            nc.vector.tensor_scalar(q_factor_20[:], rs, q_scale[:, 2:3], SHIFT_20,
                                    ALU.mult, ALU.mult).then_inc(factor_ok, 1)
            nc.vector.tensor_scalar(q_factor[:], rs, q_scale[:, 2:3], None, ALU.mult).then_inc(factor_ok, 1)
            dve.wait_ge(factor_ok, 2)

            powers, summed = {}, {}

            def power_of_two(t):
                dve.wait_ge(bits_ok, t + 1)
                m = xq_bits[:, t, :].bitcast(I32)
                powers[t] = mark(nc.vector.tensor_scalar(m, m, EXP_BITS, HALF_BIT, ALU.bitwise_and,
                                                         ALU.bitwise_or))

            def add_power(t):
                dve.wait_ge(scaled_ok, t + 1)
                need(powers[t])
                summed[t] = mark(nc.vector.scalar_tensor_tensor(
                    out=y_sb[:, t, :], in0=xq_bits[:, t, :], scalar=ROUND_MIN, in1=y_sb[:, t, :],
                    op0=ALU.max, op1=ALU.add))

            def take_power(t):
                need(summed[t])
                nc.vector.scalar_tensor_tensor(out=hn_sb[:, t, :], in0=xq_bits[:, t, :], scalar=ROUND_MIN,
                                               in1=y_sb[:, t, :], op0=ALU.max, op1=ALU.subtract,
                                               reverse1=True).then_inc(xq_ok, 1)

            nc.vector.tensor_scalar(y_sb[:, 0, :], hn_sb[:, 0, :], q_factor[:, 0:1], None,
                                    ALU.mult).then_inc(scaled_ok, 1)
            power_of_two(0)
            for t in range(TILES):
                add_power(t)
                if t + 1 < TILES:
                    power_of_two(t + 1)
                take_power(t)
            for t in range(1, TILES, 2):
                dve.wait_ge(y_ps, t + 1)
                nc.vector.tensor_copy(h_sb[:, t, :], acc[t][0:TR, :]).then_inc(y_odd_ok, 1)


def kernel(**inputs):
    import numpy as _np
    import concourse.bacc as _bacc
    from concourse import mybir as _mybir
    from concourse.bass_utils import run_bass_kernel_spmd as _run

    a = {k: _np.asarray(v) for k, v in inputs.items()}
    c = _np.ascontiguousarray
    x = a["x"]

    def chunked(w):
        return w.reshape(w.shape[0] // 128, 128, w.shape[1]).transpose(1, 0, 2)

    def head_in(w):
        return w.reshape(HEADS, E, KD, 128).transpose(0, 3, 2, 1).reshape(HEADS, 128, KD * E)

    heads = _np.concatenate([head_in(a["L0_attn_W_Q"]), head_in(a["L0_attn_W_K"]),
                             head_in(a["L0_attn_W_V"]), a["L0_attn_W_O"].transpose(0, 2, 1)], axis=2)
    r = _np.arange(TR)
    own = (r[:, None] // PATCHES) == (r[None, :] // PATCHES)
    later = r[None, :] > r[:, None]
    mask = _np.where(own, _np.where(later, -1e9, 0.0), -1e30).astype(_np.float32)
    arrays = {
        "patches": c(x[:, :PATCHES * 16, :]).reshape(TILES, TR, IN_DIM),
        "tok_w": c(chunked(a["L0_tok_W"])),
        "heads_w": c(heads),
        "ffn_w": c(chunked(a["L0_ffn_weight"].T)),
        "tok_g1": c(a["L0_tok_g1"].reshape(KIN, 128).T),
        "tok_b1": c(a["L0_tok_b1"].reshape(KIN, 128).T),
        "tok_b": a["L0_tok_b"].reshape(1, D),
        "tok_g2": a["L0_tok_g2"].reshape(1, D),
        "tok_b2": a["L0_tok_b2"].reshape(1, D),
        "ffn_scale": a["L0_ffn_weight_scale"].reshape(1, 1),
        "ffn_bias": a["L0_ffn_bias"].reshape(1, D),
        "mask": c(_np.tile(mask, (1, TILES))),
        "ident": _np.eye(128, dtype=_np.float32),
    }
    nc = _bacc.Bacc("TRN2", target_bir_lowering=False, num_devices=1)
    args = [nc.dram_tensor(n, v.shape, _mybir.dt.from_np(v.dtype), kind="ExternalInput").ap()
            for n, v in arrays.items()]
    out = nc.dram_tensor("out", (TILES, TR, D), _mybir.dt.float32, kind="ExternalOutput").ap()
    audio_tower(nc, *args, out)
    res = _run(nc, [arrays], core_ids=[0])
    return res.results[0]["out"].reshape(BATCH, PATCHES, D)
```

```python
import math
from contextlib import ExitStack

import concourse.bass as bass
from concourse import mybir

ALU = mybir.AluOpType
ACT = mybir.ActivationFunctionType
AX = mybir.AxisListType
F32 = mybir.dt.float32
F32R = mybir.dt.float32r
I32 = mybir.dt.int32

BATCH, PATCHES = 64, 7
ROWS = BATCH * PATCHES
IN_DIM = 1024
D = 512
HEADS, E = 16, 128
TILES = 4
TR = ROWS // TILES
KIN = IN_DIM // 128
KD = D // 128
QKV = 3 * KD * E
WCOLS = QKV + D
SCALE = 1.0 / math.sqrt(E)
LN_EPS, NORM_EPS = 1e-6, 1e-5
ROOTS = {0: LN_EPS, 2 * TILES + 1: NORM_EPS, TILES + 2: LN_EPS, 2 * TILES + 2: NORM_EPS,
         TILES + 3: LN_EPS, 2 * TILES + 3: NORM_EPS}
TOKW_PIECES = ((0, 2), (2, 4), (4, 6), (6, 8))
PIECES = ((0, slice(0, D // 2)), (0, slice(D // 2, D))) + tuple((t, slice(0, D)) for t in range(1, TILES))
RESULTS = tuple((t, slice(0, D)) for t in range(TILES - 1)) + ((TILES - 1, slice(0, D // 2)),
                                                               (TILES - 1, slice(D // 2, D)))
B_LO = 32
WARM_START, WARM_STREAM, WARM_LAST_TILE, WARM_NORM, WARM_SCALE, WARM_PIECE = 14, 5, 2, 27, 15, 2
FP8_MAX, SCALE_EPS = 448.0, 1e-7
EXP_BITS, HALF_BIT = 0x7F800000, 0x00400000
SHIFT_20 = 2.0 ** 20
ROUND_MIN = 1.5 * 2.0 ** (20 - 6)
NEWTON_SCALE = 2.0 ** 26
NEWTON_STEPS = (3.0, 12.0, 768.0)
RSQRT_SEED = float(0x5F3759DF - 2 ** 31)


def audio_tower(nc, patches, tok_w, heads_w, ffn_w, tok_g1, tok_b1, tok_b, tok_g2, tok_b2,
                ffn_scale, ffn_bias, mask, ident, out):
    with ExitStack() as ctx:
        def sb(name, shape, dt=F32):
            return ctx.enter_context(nc.sbuf_tensor(name, shape, dt))

        def sem(name):
            return ctx.enter_context(nc.semaphore(name))

        ident_sb = sb("ident_sb", [128, 128])
        mask_sb = sb("mask_sb", [TR, TILES * TR])
        g1_col = sb("g1_col", [128, KIN])
        b1_col = sb("b1_col", [128, KIN])
        tok_b_raw = sb("tok_b_raw", [B_LO + 1, D])
        tok_b_split = sb("tok_b_split", [B_LO + 1, D], F32R)
        ffn_b_row = sb("ffn_b_row", [TR, D])
        g2_row = sb("g2_row", [TR, D])
        b2_row = sb("b2_row", [TR, D])
        ffn_scale_col = sb("ffn_scale_col", [128, 1])

        x_in = sb("x_in", [TR, TILES, IN_DIM])
        tokw_raw = sb("tokw_raw", [128, KIN, D])
        xt = sb("xt", [128, 2, KIN * TR])

        work_sb = sb("work_sb", [TR, TILES, D])
        hn_sb = sb("hn_sb", [TR, TILES, D])
        ht_hi = sb("ht_hi", [128, KD, ROWS], F32R)
        ht_lo = sb("ht_lo", [128, KD, ROWS], F32R)

        raw = sb("raw", [128, 2, WCOLS])
        qkvw_hi = [sb(f"qkvw_hi{s}", [128, 3, KD, E], F32R) for s in range(2)]
        qkvw_lo = [sb(f"qkvw_lo{s}", [128, 3, KD, E], F32R) for s in range(2)]
        outw_hi = [sb(f"outw_hi{s}", [128, D], F32R) for s in range(2)]
        outw_lo = [sb(f"outw_lo{s}", [128, D], F32R) for s in range(2)]

        q_t = sb("q_t", [128, ROWS])
        k_t = sb("k_t", [128, ROWS])
        v_t = sb("v_t", [128, ROWS])
        v_nat = sb("v_nat", [TR, TILES, E])
        prob = sb("prob", [TR, TILES, TR])
        prob_t = sb("prob_t", [TR, TILES, TR])
        z_hi = sb("z_hi", [128, TILES, TR], F32R)
        z_lo = sb("z_lo", [128, TILES, TR], F32R)
        smax = sb("smax", [TR, TILES])
        ssum = sb("ssum", [TR, TILES])
        srec = sb("srec", [TR, TILES])

        z_last_hi = sb("z_last_hi", [128, TILES, TR], F32R)
        z_last_lo = sb("z_last_lo", [128, TILES, TR], F32R)

        ffnw_raw = sb("ffnw_raw", [128, KD, D])
        ffnw_hi = sb("ffnw_hi", [128, KD, D], F32R)
        ffnw_lo = sb("ffnw_lo", [128, KD, D], F32R)
        xq_t = sb("xq_t", [128, TILES, KD * TR], F32R)
        xq_bits = x_in[:, :, 0:D]
        y_sb = x_in[:, :, D:2 * D]

        NCOL = 4 * TILES
        LAST = 3 * TILES
        stats = sb("stats", [TR, NCOL, 2, 6])
        moments = sb("moments", [TR, NCOL, 2])
        vscaled = sb("vscaled", [TR, NCOL])
        newton = sb("newton", [TR, NCOL])
        rstd = sb("rstd", [TR, NCOL])
        nmr = sb("nmr", [TR, NCOL])
        eps_4 = sb("eps_4", [TR, len(ROOTS)])
        root = sb("root", [TR, len(ROOTS)])
        last_root = sb("last_root", [TR, TILES])
        ones_sb = sb("ones_sb", [TR, TR])
        ones_r = sb("ones_r", [B_LO + 1, TR], F32R)
        tile_max = sb("tile_max", [TR, TILES])
        row_max = sb("row_max", [TR, 1])
        max_diag = sb("max_diag", [TR, TR])
        q_scale = sb("q_scale", [TR, 3])
        q_factor = sb("q_factor", [TR, TILES])
        q_factor_20 = sb("q_factor_20", [TR, TILES])

        bank = [ctx.enter_context(nc.psum_tensor(f"bank{i}", [128, 512], F32)) for i in range(4)]
        acc = [ctx.enter_context(nc.psum_tensor(f"acc{t}", [128, D], F32)) for t in range(TILES)]

        ident_landed = sem("ident_landed")
        cols_landed = sem("cols_landed")
        tok_b_landed = sem("tok_b_landed")
        tok_b_hi_ok = sem("tok_b_hi_ok")
        tok_b_lo_ok = sem("tok_b_lo_ok")
        rows_landed = sem("rows_landed")
        late_landed = sem("late_landed")
        x_landed = [sem(f"x_landed{t}") for t in range(TILES)]
        x0_rest_landed = sem("x0_rest_landed")
        tokw_landed = [sem(f"tokw_landed{i}") for i in range(len(TOKW_PIECES))]
        raw_landed = [sem(f"raw_landed{s}") for s in range(2)]
        ffnw_landed = sem("ffnw_landed")
        out_stored = sem("out_stored")

        dve_step = sem("dve_step")
        eps_ok = sem("eps_ok")
        variance_ok = sem("variance_ok")
        root_ok = sem("root_ok")
        x_scaled = sem("x_scaled")
        x0_half_normed = sem("x0_half_normed")
        x_normed = sem("x_normed")
        xt_ps = sem("xt_ps")
        xt_ok = sem("xt_ok")
        tok_ps = sem("tok_ps")
        h_ok = sem("h_ok")
        hn_scaled = sem("hn_scaled")
        hn_ok = sem("hn_ok")
        ht_ps = sem("ht_ps")
        ht_hi_ok = sem("ht_hi_ok")
        ht_lo_ok = sem("ht_lo_ok")

        qkvw_hi_ok = sem("qkvw_hi_ok")
        qkvw_lo_ok = sem("qkvw_lo_ok")
        outw_hi_ok = sem("outw_hi_ok")
        outw_lo_ok = sem("outw_lo_ok")
        q_ps, k_ps, v_ps = sem("q_ps"), sem("k_ps"), sem("v_ps")
        q_ok, k_ok, vt_ok = sem("q_ok"), sem("k_ok"), sem("vt_ok")
        s_ps = sem("s_ps")
        s_read = sem("s_read")
        shifted = sem("shifted")
        exp_ok = sem("exp_ok")
        prob_ok = sem("prob_ok")
        pt_ps, pt_ok = sem("pt_ps"), sem("pt_ok")
        vn_ps, vn_ok = sem("vn_ps"), sem("vn_ok")
        z_ps, z_hi_ok, z_lo_ok = sem("z_ps"), sem("z_hi_ok"), sem("z_lo_ok")
        o_ps = sem("o_ps")
        softmax_step = sem("softmax_step")

        ffnw_scaled = sem("ffnw_scaled")
        ffnw_hi_ok = sem("ffnw_hi_ok")
        ffnw_lo_ok = sem("ffnw_lo_ok")
        ones_ok = sem("ones_ok")
        mean_ok = sem("mean_ok")
        magnitude_ok = sem("magnitude_ok")
        centred = sem("centred")
        last_root_ok = sem("last_root_ok")
        diag_ok = sem("diag_ok")
        max_ps = sem("max_ps")
        factor_ok = sem("factor_ok")
        bits_ok = sem("bits_ok")
        scaled_ok = sem("scaled_ok")
        xq_ok = sem("xq_ok")
        xqt_ps = sem("xqt_ps")
        xqt_ok = sem("xqt_ok")
        y_ps = sem("y_ps")
        y_ok = sem("y_ok")

        ht_bank = (bank[0], bank[1], bank[3], bank[3])
        block = ctx.enter_context(nc.Block())

        def flat_ffnw(w):
            return w[:].rearrange("p k n -> p (k n)")

        def loop_heads(eng, step):
            with eng.Fori(0, (HEADS - 2) // 2) as i:
                step(i * 2 + 1, i, 1)
                step(i * 2 + 2, i + 1, 0)

        @block.sync
        def _(sp):
            def load(dst, src, landed):
                sp.dma_start(dst, src).then_inc(landed, 16)

            def load_tokw(i):
                a, b = TOKW_PIECES[i]
                load(tokw_raw[:, a:b, :], tok_w[:, a:b, :], tokw_landed[i])

            for c, landed in ((slice(0, 512), x_landed[0]), (slice(512, IN_DIM), x0_rest_landed)):
                load(x_in[:, 0, c], patches[0][:, c], landed)
            load(ident_sb[:], ident, ident_landed)
            load(g1_col[:], tok_g1, cols_landed)
            load(b1_col[:], tok_b1, cols_landed)
            load(x_in[:, 1, :], patches[1], x_landed[1])
            load_tokw(0)
            load_tokw(1)
            load(x_in[:, 2, :], patches[2], x_landed[2])
            load(tok_b_raw[:], tok_b, tok_b_landed)
            load_tokw(2)
            load_tokw(3)
            load(x_in[:, 3, :], patches[3], x_landed[3])
            load(g2_row[:], tok_g2.to_broadcast([TR, D]), rows_landed)
            load(b2_row[:], tok_b2.to_broadcast([TR, D]), rows_landed)
            load(mask_sb[:], mask, late_landed)
            load(ffn_scale_col[:], ffn_scale.to_broadcast([128, 1]), late_landed)
            load(ffn_b_row[:], ffn_bias.to_broadcast([TR, D]), late_landed)
            for s in range(2):
                sp.dma_start(raw[:, s, :], heads_w[s]).then_inc(raw_landed[s], 16)
            sp.dma_start(ffnw_raw[:], ffn_w).then_inc(ffnw_landed, 16)

            def load_head(h, _, s):
                sp.wait_ge(outw_hi_ok, h)
                sp.wait_ge(outw_lo_ok, h)
                sp.dma_start(raw[:, 1 - s, :], heads_w[h + 1]).then_inc(raw_landed[1 - s], 16)

            loop_heads(sp, load_head)
            for i, (t, c) in enumerate(RESULTS):
                sp.wait_ge(y_ok, i + 1)
                sp.dma_start(out[t][:, c], work_sb[:, t, c]).then_inc(out_stored, 16)
            sp.wait_ge(out_stored, 16 * len(RESULTS))

        @block.tensor
        def _(pe):
            def split_product(ps, hi, lo, whi, wlo, first, last):
                nc.tensor.matmul(ps, hi, whi, start=first, stop=False, skip_group_check=True)
                nc.tensor.matmul(ps, hi, wlo, start=False, stop=False, skip_group_check=True)
                return nc.tensor.matmul(ps, lo, whi, start=False, stop=last, skip_group_check=True)

            def keep_warm(n, ps):
                for _ in range(n):
                    nc.tensor.matmul(ps[0:TR, 0:TR], ones_sb[:], ones_sb[:], start=True, stop=True,
                                     skip_group_check=True)

            def patch_transposes(t):
                if t == 0:
                    pe.wait_ge(ident_landed, 16)
                    pe.wait_ge(x0_half_normed, 1)
                else:
                    pe.wait_ge(x_normed, t + 1)
                if t >= 2:
                    pe.wait_ge(xt_ok, KIN * (t - 1))
                for k in range(KIN):
                    if t == 0 and k == KIN // 2:
                        pe.wait_ge(x_normed, 1)
                    b = 2 * (t % 2) + k // 4
                    mm = nc.tensor.transpose(bank[b][:, k % 4 * TR:(k % 4 + 1) * TR],
                                             x_in[:, t, k * 128:(k + 1) * 128], ident_sb[0:TR, 0:TR])
                    if k % 4 == 3:
                        mm.then_inc(xt_ps, 1)

            def embed(t, half):
                for k in range(half * KIN // 2, (half + 1) * KIN // 2):
                    for i, (first_chunk, _) in enumerate(TOKW_PIECES):
                        if t == 0 and k == first_chunk:
                            pe.wait_ge(tokw_landed[i], 16)
                    pe.wait_ge(xt_ok, KIN * t + k + 1)
                    nc.tensor.matmul(acc[t][0:TR, :], xt[:, t % 2, k * TR:(k + 1) * TR], tokw_raw[:, k, :],
                                     start=(k == 0), stop=False, skip_group_check=True)
                if half == 1:
                    if t == 0:
                        pe.wait_ge(tok_b_lo_ok, 1)
                    nc.tensor.matmul(acc[t][0:TR, :], ones_r[:], tok_b_split[:], start=False, stop=True,
                                     skip_group_check=True).then_inc(tok_ps, 1)

            def stream_transposes(t):
                pe.wait_ge(hn_ok, t + 1)
                if t <= 1:
                    pe.wait_ge(xt_ok, KIN * (TILES - 1))
                if t == 2:
                    pe.wait_ge(xt_ok, KIN * TILES)
                for k in range(KD):
                    last = nc.tensor.transpose(ht_bank[t][:, k * TR:(k + 1) * TR],
                                               hn_sb[:, t, k * 128:(k + 1) * 128], ident_sb[0:TR, 0:TR])
                last.then_inc(ht_ps, 1)

            pe.wait_ge(ones_ok, 2)
            keep_warm(WARM_START, acc[TILES - 1])
            patch_transposes(0)
            for t in range(TILES):
                embed(t, 0)
                if t + 1 < TILES:
                    patch_transposes(t + 1)
                else:
                    stream_transposes(1)
                embed(t, 1)
                if t == TILES - 2:
                    stream_transposes(0)
            stream_transposes(2)
            keep_warm(WARM_STREAM, bank[2])

            def project(which, ps, s, done=None, rows=slice(0, ROWS), chunks=range(KD)):
                for k in chunks:
                    wh, wl = qkvw_hi[s][:, which, k, :], qkvw_lo[s][:, which, k, :]
                    last = split_product(ps[:, rows], wh, wl, ht_hi[:, k, rows], ht_lo[:, k, rows],
                                         k == 0, k == KD - 1)
                if done is not None:
                    last.then_inc(done, 1)

            def project_q(h, s):
                pe.wait_ge(qkvw_hi_ok, h + 1)
                pe.wait_ge(qkvw_lo_ok, h + 1)
                project(0, bank[0], s, q_ps)

            def project_v(h, s):
                pe.wait_ge(q_ok, h + 1)
                project(2, bank[0], s, v_ps)

            def prob_transposes(h):
                pe.wait_ge(prob_ok, h + 1)
                pe.wait_ge(vn_ok, h + 1)
                for t in range(TILES):
                    last = nc.tensor.transpose(bank[3][0:TR, t * TR:(t + 1) * TR], prob[:, t, :],
                                               ident_sb[0:TR, 0:TR])
                last.then_inc(pt_ps, 1)

            def weigh_values(h, b=2):
                pe.wait_ge(pt_ok, h + 1)
                for t in range(TILES):
                    last = nc.tensor.matmul(bank[b][:, t * TR:(t + 1) * TR], v_nat[:, t, :],
                                            prob_t[:, t, :], start=True, stop=True)
                last.then_inc(z_ps, 1)

            def scores(h):
                pe.wait_ge(k_ok, h + 1)
                for t in range(TILES):
                    c = slice(t * TR, (t + 1) * TR)
                    last = nc.tensor.matmul(bank[1][0:TR, c], q_t[:, c], k_t[:, c], start=True, stop=True)
                last.then_inc(s_ps, 1)

            def value_transposes(h):
                pe.wait_ge(vt_ok, h + 1)
                for t in range(TILES):
                    last = nc.tensor.transpose(bank[3][0:TR, t * E:(t + 1) * E],
                                               v_t[:, t * TR:(t + 1) * TR], ident_sb[:])
                last.then_inc(vn_ps, 1)

            def project_out(h, s):
                pe.wait_ge(outw_hi_ok, h + 1)
                pe.wait_ge(outw_lo_ok, h + 1)
                pe.wait_ge(z_hi_ok, h + 1)
                for t in range(TILES):
                    for w in (outw_hi[s], outw_lo[s]):
                        nc.tensor.matmul(acc[t][0:TR, :], z_hi[:, t, :], w[:], start=False, stop=False,
                                         skip_group_check=True)
                pe.wait_ge(z_lo_ok, h + 1)
                for t in range(TILES):
                    last = nc.tensor.matmul(acc[t][0:TR, :], z_lo[:, t, :], outw_hi[s][:], start=False,
                                            stop=False, skip_group_check=True)
                last.then_inc(o_ps, 1)

            def head_step(h, _, s):
                project_q(h, s)
                pe.wait_ge(s_read, h)
                project(1, bank[1], s, k_ps)
                prob_transposes(h - 1)
                project_v(h, s)
                weigh_values(h - 1)
                scores(h)
                value_transposes(h)
                project_out(h - 1, 1 - s)

            pe.wait_ge(qkvw_hi_ok, 1)
            pe.wait_ge(qkvw_lo_ok, 1)
            pe.wait_ge(ht_hi_ok, 3)
            pe.wait_ge(ht_lo_ok, 3)
            first_part, last_part = slice(0, 3 * TR), slice(3 * TR, ROWS)
            project(0, bank[0], 0, o_ps, rows=first_part)
            project(1, bank[1], 0, rows=first_part)
            keep_warm(WARM_LAST_TILE, bank[2])
            stream_transposes(3)
            project(2, bank[2], 0, rows=first_part)
            pe.wait_ge(ht_hi_ok, TILES)
            pe.wait_ge(ht_lo_ok, TILES)
            for which, done in enumerate((q_ps, k_ps, v_ps)):
                project(which, bank[which], 0, done, rows=last_part)
            pe.wait_ge(q_ok, 1)
            scores(0)
            value_transposes(0)

            loop_heads(pe, head_step)

            h, s = HEADS - 1, (HEADS - 1) % 2
            project_q(h, s)
            pe.wait_ge(s_read, h)
            project(1, bank[1], s, k_ps)
            prob_transposes(h - 1)
            pe.wait_ge(q_ok, h + 1)
            project(2, bank[0], s, chunks=range(1))
            scores(h)
            project(2, bank[0], s, v_ps, chunks=range(1, KD))
            weigh_values(h - 1)
            value_transposes(h)
            pe.wait_ge(outw_hi_ok, h)
            pe.wait_ge(outw_lo_ok, h)
            pe.wait_ge(z_hi_ok, h)
            for z, w, after in ((z_hi, outw_hi, prob_transposes), (z_hi, outw_lo, weigh_values),
                                (z_lo, outw_hi, None)):
                if z is z_lo:
                    pe.wait_ge(z_lo_ok, h)
                for t in range(TILES):
                    last = nc.tensor.matmul(acc[t][0:TR, :], z[:, t, :], w[1 - s][:], start=False, stop=False,
                                            skip_group_check=True)
                if after is prob_transposes:
                    after(h)
                elif after is weigh_values:
                    after(h, 0)
            last.then_inc(o_ps, 1)
            pe.wait_ge(outw_hi_ok, h + 1)
            pe.wait_ge(outw_lo_ok, h + 1)
            pe.wait_ge(z_hi_ok, h + 1)
            for t in range(TILES):
                for z, w in ((z_last_hi, outw_hi), (z_last_hi, outw_lo), (z_last_lo, outw_hi)):
                    if t == 0 and z is z_last_lo:
                        pe.wait_ge(z_lo_ok, h + 1)
                    last = nc.tensor.matmul(acc[t][0:TR, :], z[:, t, :], w[s][:], start=False,
                                            stop=z is z_last_lo, skip_group_check=True)
                last.then_inc(o_ps, 1)

            keep_warm(WARM_NORM, bank[0])
            pe.wait_ge(diag_ok, 1)
            nc.tensor.matmul(bank[1][0:TR, 0:TR], ones_sb[:], max_diag[:], start=True,
                             stop=True).then_inc(max_ps, 1)
            keep_warm(WARM_SCALE, bank[0])
            pe.wait_ge(ffnw_hi_ok, 1)
            pe.wait_ge(ffnw_lo_ok, 1)

            def quantised_transposes(p):
                t, cols = PIECES[p]
                pe.wait_ge(xq_ok, p + 1)
                if p == 3:
                    pe.wait_ge(factor_ok, 1)
                if p >= 4:
                    pe.wait_ge(xqt_ok, p - 3)
                for k in range(cols.start // 128, cols.stop // 128):
                    last = nc.tensor.transpose(bank[(p + 2) % 4][:, k * TR:(k + 1) * TR],
                                               hn_sb[:, t, k * 128:(k + 1) * 128], ident_sb[0:TR, 0:TR])
                last.then_inc(xqt_ps, 1)

            def feed_forward(p):
                t, cols = PIECES[p]
                pe.wait_ge(xqt_ok, p + 1)
                for k in range(cols.start // 128, cols.stop // 128):
                    for w in (ffnw_hi, ffnw_lo):
                        last = nc.tensor.matmul(acc[t][0:TR, :], xq_t[:, t, k * TR:(k + 1) * TR], w[:, k, :],
                                                start=False, stop=(k == KD - 1 and w is ffnw_lo),
                                                skip_group_check=True)
                if k == KD - 1:
                    last.then_inc(y_ps, 1)

            quantised_transposes(0)
            keep_warm(WARM_PIECE, bank[0])
            quantised_transposes(1)
            feed_forward(0)
            quantised_transposes(2)
            feed_forward(1)
            quantised_transposes(3)
            feed_forward(2)
            quantised_transposes(4)
            feed_forward(3)
            feed_forward(4)

        @block.scalar
        def _(act):
            def hi_part(dst, src):
                return nc.scalar.copy(dst, src)

            def take_root(c):
                i = list(ROOTS).index(c)
                act.wait_ge(variance_ok, i + 1)
                act.wait_ge(eps_ok, len(ROOTS))
                nc.scalar.activation(root[:, i:i + 1], moments[:, c, 1:2], ACT.Sqrt, bias=eps_4[:, i:i + 1],
                                     scale=4.0).then_inc(root_ok, 1)

            def normalise(t, c=slice(0, IN_DIM)):
                act.wait_ge(x_scaled, t + 1)
                nc.scalar.activation(x_in[:, t, c], x_in[:, t, c], ACT.Identity, bias=nmr[:, t:t + 1],
                                     scale=rstd[:, t:t + 1]).then_inc(x_normed, 1)

            def patch_evacuate(t):
                for half in range(2):
                    act.wait_ge(xt_ps, 2 * t + half + 1)
                    if t >= 2 and half == 0:
                        act.wait_ge(tok_ps, t - 1)
                    for k in range(half * KIN // 2, (half + 1) * KIN // 2):
                        nc.scalar.activation(xt[:, t % 2, k * TR:(k + 1) * TR],
                                             bank[2 * (t % 2) + half][:, k % 4 * TR:(k % 4 + 1) * TR],
                                             ACT.Identity, bias=b1_col[:, k:k + 1],
                                             scale=g1_col[:, k:k + 1]).then_inc(xt_ok, 1)

            def normalise_stream(t):
                c = 2 * TILES + t
                act.wait_ge(hn_scaled, t + 1)
                act.wait_ge(h_ok, t + 1)
                nc.scalar.activation(hn_sb[:, t, :], acc[t][0:TR, :], ACT.Identity, bias=nmr[:, c:c + 1],
                                     scale=rstd[:, c:c + 1]).then_inc(hn_ok, 1)

            def stream_evacuate(t):
                act.wait_ge(ht_ps, t + 1)
                hi_part(ht_hi[:, :, t * TR:(t + 1) * TR],
                        ht_bank[t][:, 0:KD * TR].rearrange("p (k r) -> p k r", k=KD)).then_inc(ht_hi_ok, 1)

            def split_qkv(h, r, s):
                act.wait_ge(raw_landed[s], (r + 1) * 16)
                hi_part(qkvw_hi[s][:].rearrange("p a k e -> p (a k e)"),
                        raw[:, s, 0:QKV]).then_inc(qkvw_hi_ok, 1)

            def split_out(h, s):
                hi_part(outw_hi[s][:], raw[:, s, QKV:WCOLS]).then_inc(outw_hi_ok, 1)

            take_root(0)
            normalise(0, slice(IN_DIM // 2, IN_DIM))
            act.wait_ge(cols_landed, 32)
            patch_evacuate(0)
            normalise(1)
            act.wait_ge(tok_b_landed, 16)
            hi_part(tok_b_split[:], tok_b_raw[:]).then_inc(tok_b_hi_ok, 1)
            patch_evacuate(1)
            normalise(2)
            normalise(3)
            patch_evacuate(2)
            split_qkv(0, 0, 0)
            split_qkv(1, 0, 1)
            split_out(0, 0)
            normalise_stream(0)
            patch_evacuate(3)
            take_root(2 * TILES + 1)
            stream_evacuate(0)
            normalise_stream(1)
            take_root(TILES + 2)
            stream_evacuate(1)
            take_root(2 * TILES + 2)
            normalise_stream(2)
            stream_evacuate(2)
            take_root(TILES + 3)
            take_root(2 * TILES + 3)
            stream_evacuate(3)
            nc.scalar.activation(root[:, 0:1], eps_4[:, 0:1], ACT.Exp)

            def exponentiate(h):
                act.wait_ge(shifted, h + 1)
                nc.scalar.activation(prob[:], prob[:], ACT.Exp).then_inc(exp_ok, 1)

            def copy_probs(h):
                act.wait_ge(pt_ps, h + 1)
                nc.scalar.copy(prob_t[:].rearrange("p t r -> p (t r)"),
                               bank[3][0:TR, 0:ROWS]).then_inc(pt_ok, 1)

            def copy_q(h):
                act.wait_ge(q_ps, h + 1)
                nc.scalar.copy(q_t[:], bank[0][:, 0:ROWS]).then_inc(q_ok, 1)

            def copy_k(h):
                act.wait_ge(k_ps, h + 1)
                nc.scalar.copy(k_t[:], bank[1][:, 0:ROWS]).then_inc(k_ok, 1)

            def copy_v(h, b=0):
                act.wait_ge(v_ps, h + 1)
                nc.scalar.copy(v_t[:], bank[b][:, 0:ROWS]).then_inc(vt_ok, 1)

            def copy_v_rows(h):
                act.wait_ge(vn_ps, h + 1)
                nc.scalar.copy(v_nat[:].rearrange("p t e -> p (t e)"), bank[3][0:TR, :]).then_inc(vn_ok, 1)

            def values_hi(h, z_hi=z_hi, b=2):
                act.wait_ge(z_ps, h + 1)
                hi_part(z_hi[:].rearrange("p t r -> p (t r)"), bank[b][:, 0:ROWS]).then_inc(z_hi_ok, 1)

            def head_step(h, r, s):
                exponentiate(h - 1)
                act.wait_ge(o_ps, h)
                split_out(h, s)
                copy_q(h)
                act.wait_ge(v_ps, h)
                split_qkv(h + 1, r if s == 0 else r + 1, 1 - s)
                copy_k(h)
                copy_probs(h - 1)
                copy_v(h)
                values_hi(h - 1)
                copy_v_rows(h)

            copy_q(0)
            copy_k(0)
            copy_v(0, 2)
            copy_v_rows(0)

            loop_heads(act, head_step)

            h, s = HEADS - 1, (HEADS - 1) % 2
            exponentiate(h - 1)
            act.wait_ge(o_ps, h)
            split_out(h, s)
            copy_q(h)
            copy_k(h)
            copy_probs(h - 1)
            act.wait_ge(ffnw_scaled, 1)
            hi_part(flat_ffnw(ffnw_hi), flat_ffnw(ffnw_raw)).then_inc(ffnw_hi_ok, 1)
            copy_v(h)
            exponentiate(h)
            values_hi(h - 1)
            copy_v_rows(h)
            copy_probs(h)
            values_hi(h, z_last_hi, 0)
            nc.scalar.activation(root[:, 0:1], eps_4[:, 0:1], ACT.Sqrt)

            for t in range(TILES):
                act.wait_ge(mean_ok, t + 1)
                nc.scalar.activation(hn_sb[:, t, :], acc[t][0:TR, :], ACT.Identity,
                                     bias=moments[:, LAST + t, 0:1], scale=-1.0).then_inc(centred, 1)
            act.wait_ge(mean_ok, TILES)
            nc.scalar.activation(last_root[:], moments[:, LAST:LAST + TILES, 1], ACT.Sqrt, bias=eps_4[:, 1:2],
                                 scale=4.0).then_inc(last_root_ok, 1)

            def magnitudes(p):
                t, c = PIECES[p]
                nc.scalar.mul(xq_bits[:, t, c], hn_sb[:, t, c], q_factor_20[:, t:t + 1]).then_inc(bits_ok, 1)

            def scaled(p):
                t, c = PIECES[p]
                nc.scalar.mul(y_sb[:, t, c], hn_sb[:, t, c], q_factor[:, t:t + 1]).then_inc(scaled_ok, 1)

            def quantised_evacuate(p):
                t, c = PIECES[p]
                c = slice(c.start // 128 * TR, c.stop // 128 * TR)
                act.wait_ge(xqt_ps, p + 1)
                hi_part(xq_t[:, t, c], bank[(p + 2) % 4][:, c]).then_inc(xqt_ok, 1)

            act.wait_ge(factor_ok, 2)
            act.wait_ge(centred, TILES)
            magnitudes(0)
            magnitudes(1)
            magnitudes(2)
            scaled(2)
            quantised_evacuate(0)
            magnitudes(3)
            scaled(3)
            quantised_evacuate(1)
            magnitudes(4)
            quantised_evacuate(2)
            scaled(4)
            quantised_evacuate(3)
            quantised_evacuate(4)

        @block.vector
        def _(dve):
            steps = [0]

            def mark(ins):
                steps[0] += 1
                ins.then_inc(dve_step, 1)
                return steps[0]

            def need(step):
                dve.wait_ge(dve_step, step)

            def link(ins):
                need(mark(ins))

            def lo_part(dst, src, hi):
                return nc.vector.tensor_tensor(dst, src, hi.bitcast(F32), ALU.subtract)

            def moments_of(c, parts, rest_landed=None):
                for i, p in enumerate(parts):
                    if i == 1 and rest_landed is not None:
                        dve.wait_ge(rest_landed, 16)
                    last = nc.vector.bn_stats(stats[:, c, i, :], p)
                link(last)
                aggregate = nc.vector.bn_aggr(moments[:, c, :], stats[:, c, 0:len(parts), :])
                if c not in ROOTS:
                    return mark(aggregate)
                aggregate.then_inc(variance_ok, 1)

            def need_moments(c, step):
                if c in ROOTS:
                    dve.wait_ge(variance_ok, list(ROOTS).index(c) + 1)
                else:
                    need(step)

            def rsqrt_from_root(c, between=None):
                i = list(ROOTS).index(c)
                v, y, n = vscaled[:, c:c + 1], rstd[:, c:c + 1], newton[:, c:c + 1]
                minus_v4 = mark(nc.vector.tensor_scalar(v, moments[:, c, 1:2], ROOTS[c], -4.0,
                                                        ALU.add, ALU.mult))
                if between is not None:
                    between(0)
                dve.wait_ge(root_ok, i + 1)
                link(nc.vector.reciprocal(y, root[:, i:i + 1]))
                if between is not None:
                    between(1)
                need(minus_v4)
                link(nc.vector.tensor_scalar(n, y, y, v, ALU.mult, ALU.mult))
                return mark(nc.vector.scalar_tensor_tensor(out=y, in0=n, scalar=3.0, in1=y,
                                                           op0=ALU.add, op1=ALU.mult))

            def rsqrt(columns, moments_step, between=None):
                if len(columns) == 1 and columns[0][0] in ROOTS:
                    need_moments(columns[0][0], moments_step)
                    return rsqrt_from_root(columns[0][0], between)
                done = {c: moments_step for c, _ in columns}
                for i in range(2 + 2 * len(NEWTON_STEPS)):
                    for c, eps in columns:
                        v, y, n = vscaled[:, c:c + 1], rstd[:, c:c + 1], newton[:, c:c + 1]
                        need(done[c])
                        if i == 0:
                            ins = nc.vector.tensor_scalar(v, moments[:, c, 1:2], eps, NEWTON_SCALE,
                                                          ALU.add, ALU.mult)
                        elif i == 1:
                            ins = nc.vector.tensor_scalar(y.bitcast(I32), v.bitcast(I32), -0.5, RSQRT_SEED,
                                                          ALU.mult, ALU.add)
                        elif i % 2 == 0:
                            ins = nc.vector.tensor_scalar(n, y, y, v, ALU.mult, ALU.mult)
                        else:
                            ins = nc.vector.scalar_tensor_tensor(out=y, in0=n, scalar=NEWTON_STEPS[i // 2 - 1],
                                                                 in1=y, op0=ALU.subtract, op1=ALU.mult)
                        done[c] = mark(ins)
                    if between is not None:
                        between(i)
                return max(done.values())

            def negative_mean_scaled(c):
                return nc.vector.scalar_tensor_tensor(out=nmr[:, c:c + 1], in0=moments[:, c, 0:1],
                                                      scalar=-1.0, in1=rstd[:, c:c + 1],
                                                      op0=ALU.mult, op1=ALU.mult)

            def patch_moments(t):
                dve.wait_ge(x_landed[t], 16)
                return moments_of(t, [x_in[:, t, i * 512:(i + 1) * 512] for i in range(IN_DIM // 512)],
                                  x0_rest_landed if t == 0 else None)

            def stream_lo(t):
                dve.wait_ge(ht_hi_ok, t + 1)
                c = slice(t * TR, (t + 1) * TR)
                lo_part(ht_lo[:, :, c], ht_bank[t][:, 0:KD * TR].rearrange("p (k r) -> p k r", k=KD),
                        ht_hi[:, :, c]).then_inc(ht_lo_ok, 1)

            stream_step = {}

            def stream_norms(t, own, between=None, patch=None):
                columns, step = [], 0
                if t is not None:
                    c = TILES + t
                    dve.wait_ge(tok_ps, t + 1)
                    step = moments_of(c, [acc[t][0:TR, :]])
                    need_moments(c, step)
                    centred_step = mark(nc.vector.scalar_tensor_tensor(
                        out=work_sb[:, t, :], in0=acc[t][0:TR, :], scalar=moments[:, c, 0:1], in1=g2_row[:],
                        op0=ALU.subtract, op1=ALU.mult))
                    columns.append((c, LN_EPS))
                if patch is not None:
                    step = max(step, patch[1])
                    columns.append((patch[0], LN_EPS))
                if own is not None:
                    step = max(s for s in (step, stream_step[own], 0) if s is not None)
                    columns.append((2 * TILES + own, NORM_EPS))
                need(rsqrt(columns, step, between))
                if patch is not None:
                    negative_mean_scaled(patch[0]).then_inc(x_scaled, 1)
                if own is not None and own < TILES - 1:
                    negative_mean_scaled(2 * TILES + own).then_inc(hn_scaled, 1)
                elif own is not None:
                    p = 2 * TILES + own
                    nc.vector.tensor_scalar(hn_sb[:, own, :], acc[own][0:TR, :], moments[:, p, 0:1],
                                            rstd[:, p:p + 1], ALU.subtract, ALU.mult).then_inc(hn_ok, 1)
                if t is not None:
                    need(centred_step)
                    nc.vector.scalar_tensor_tensor(out=acc[t][0:TR, :], in0=work_sb[:, t, :],
                                                   scalar=rstd[:, c:c + 1], in1=b2_row[:],
                                                   op0=ALU.mult, op1=ALU.add).then_inc(h_ok, 1)
                if t is not None:
                    dve.wait_ge(h_ok, t + 1)
                    stream_step[t] = moments_of(2 * TILES + t, [acc[t][0:TR, :]])

            def split_qkv(h, s):
                dve.wait_ge(qkvw_hi_ok, h + 1)
                lo_part(qkvw_lo[s][:].rearrange("p a k e -> p (a k e)"), raw[:, s, 0:QKV],
                        qkvw_hi[s][:].rearrange("p a k e -> p (a k e)")).then_inc(qkvw_lo_ok, 1)

            def split_out(h, s):
                dve.wait_ge(outw_hi_ok, h + 1)
                lo_part(outw_lo[s][:], raw[:, s, QKV:WCOLS], outw_hi[s][:]).then_inc(outw_lo_ok, 1)

            nc.vector.memset(ones_sb[:], 1.0).then_inc(ones_ok, 1)
            nc.vector.memset(ones_r[:].bitcast(F32), 1.0).then_inc(ones_ok, 1)
            for i, eps in enumerate(ROOTS.values()):
                nc.vector.memset(eps_4[:, i:i + 1], 4.0 * eps).then_inc(eps_ok, 1)
            need(rsqrt([(0, LN_EPS)], patch_moments(0)))
            negative_mean_scaled(0).then_inc(x_scaled, 1)
            nc.vector.tensor_scalar(x_in[:, 0, 0:IN_DIM // 2], x_in[:, 0, 0:IN_DIM // 2], moments[:, 0, 0:1],
                                    rstd[:, 0:1], ALU.subtract, ALU.mult).then_inc(x0_half_normed, 1)
            need(rsqrt([(1, LN_EPS)], patch_moments(1)))
            negative_mean_scaled(1).then_inc(x_scaled, 1)

            def bias_lo():
                b = slice(B_LO, B_LO + 1)
                dve.wait_ge(tok_b_hi_ok, 1)
                lo_part(tok_b_split[b], tok_b_raw[b], tok_b_split[b]).then_inc(tok_b_lo_ok, 1)

            need(rsqrt([(2, LN_EPS)], patch_moments(2), between=lambda i: bias_lo() if i == 5 else None))
            negative_mean_scaled(2).then_inc(x_scaled, 1)
            dve.wait_ge(rows_landed, 32)
            stream_norms(0, None, patch=(3, patch_moments(3)))
            stream_norms(1, 0)
            stream_norms(None, 1, between=lambda i: split_qkv(0, 0) if i == 0 else None)
            stream_norms(2, None, between=lambda i: stream_lo(0) if i == 0 else None)
            stream_norms(None, 2)
            stream_lo(1)
            stream_norms(3, None, between=lambda i: stream_lo(2) if i == 0 else None)
            stream_norms(None, 3)
            stream_lo(3)

            flat = prob[:].rearrange("p t r -> p (t r)")

            def over_keys(col):
                return col[:, :, None].to_broadcast([TR, TILES, TR])

            def softmax_shift(h):
                dve.wait_ge(s_ps, h + 1)
                nc.vector.scalar_tensor_tensor(out=flat, in0=bank[1][0:TR, 0:ROWS], scalar=SCALE,
                                               in1=mask_sb[:], op0=ALU.mult, op1=ALU.add).then_inc(s_read, 1)
                dve.wait_ge(s_read, h + 1)
                nc.vector.tensor_reduce(smax[:], prob[:], AX.X, ALU.max).then_inc(softmax_step, 1)
                dve.wait_ge(softmax_step, h * 3 + 1)
                nc.vector.tensor_tensor(prob[:], prob[:], over_keys(smax), ALU.subtract).then_inc(shifted, 1)

            def softmax_scale(h):
                dve.wait_ge(exp_ok, h + 1)
                nc.vector.tensor_reduce(ssum[:], prob[:], AX.X, ALU.add).then_inc(softmax_step, 1)
                dve.wait_ge(softmax_step, h * 3 + 2)
                nc.vector.reciprocal(srec[:], ssum[:]).then_inc(softmax_step, 1)
                dve.wait_ge(softmax_step, h * 3 + 3)
                nc.vector.tensor_tensor(prob[:], prob[:], over_keys(srec), ALU.mult).then_inc(prob_ok, 1)

            def values_lo(h, z_hi=z_hi, z_lo=z_lo, b=2):
                dve.wait_ge(z_hi_ok, h + 1)
                lo_part(z_lo[:].rearrange("p t r -> p (t r)"), bank[b][:, 0:ROWS],
                        z_hi[:].rearrange("p t r -> p (t r)")).then_inc(z_lo_ok, 1)

            def head_step(h, r, s):
                softmax_shift(h - 1)
                softmax_scale(h - 1)
                split_out(h, s)
                split_qkv(h + 1, 1 - s)
                values_lo(h - 1)

            split_out(0, 0)
            split_qkv(1, 1)

            loop_heads(dve, head_step)

            h, s = HEADS - 1, (HEADS - 1) % 2
            softmax_shift(h - 1)
            split_out(h, s)
            softmax_scale(h - 1)
            dve.wait_ge(ffnw_landed, 16)
            dve.wait_ge(late_landed, 48)
            nc.vector.tensor_scalar(flat_ffnw(ffnw_raw), flat_ffnw(ffnw_raw), ffn_scale_col[:], None,
                                    ALU.mult).then_inc(ffnw_scaled, 1)
            dve.wait_ge(pt_ps, h)
            softmax_shift(h)
            softmax_scale(h)
            values_lo(h - 1)
            dve.wait_ge(ffnw_hi_ok, 1)
            lo_part(flat_ffnw(ffnw_lo), flat_ffnw(ffnw_raw), flat_ffnw(ffnw_hi)).then_inc(ffnw_lo_ok, 1)
            values_lo(h, z_last_hi, z_last_lo, 0)

            def magnitude(t):
                dve.wait_ge(centred, t + 1)
                nc.vector.tensor_reduce(tile_max[:, t:t + 1], hn_sb[:, t, :], AX.X, ALU.max,
                                        apply_absolute_value=True).then_inc(magnitude_ok, 1)

            def last_moments(t):
                need(taken[t])
                nc.vector.bn_aggr(moments[:, LAST + t, :], stats[:, LAST + t, 0:1, :]).then_inc(mean_ok, 1)

            taken = {}
            for t in range(TILES):
                dve.wait_ge(o_ps, HEADS + t + 1)
                taken[t] = mark(nc.vector.bn_stats(stats[:, LAST + t, 0, :], acc[t][0:TR, :]))
                if t >= 1:
                    last_moments(t - 1)
                if t >= 2:
                    magnitude(t - 2)
            last_moments(TILES - 1)
            dve.wait_ge(mean_ok, TILES)
            c = slice(LAST, LAST + TILES)
            v, rs, n = vscaled[:, c], rstd[:, c], newton[:, c]
            minus_v4 = mark(nc.vector.tensor_scalar(v, moments[:, c, 1], NORM_EPS, -4.0, ALU.add, ALU.mult))
            magnitude(2)
            dve.wait_ge(last_root_ok, 1)
            link(nc.vector.reciprocal(rs, last_root[:]))
            square = mark(nc.vector.tensor_tensor(n, rs, rs, ALU.mult))
            magnitude(3)
            need(max(square, minus_v4))
            link(nc.vector.tensor_tensor(n, n, v, ALU.mult))
            link(nc.vector.scalar_tensor_tensor(out=rs, in0=n, scalar=3.0, in1=rs,
                                                op0=ALU.add, op1=ALU.mult))
            dve.wait_ge(magnitude_ok, TILES)
            link(nc.vector.tensor_tensor(tile_max[:], tile_max[:], rs, ALU.mult))
            link(nc.vector.tensor_reduce(row_max[:], tile_max[:], AX.X, ALU.max))
            nc.vector.tensor_scalar(max_diag[:], ident_sb[0:TR, 0:TR], row_max[:], None,
                                    ALU.mult).then_inc(diag_ok, 1)
            dve.wait_ge(max_ps, 1)
            link(nc.vector.tensor_reduce(q_scale[:, 0:1], bank[1][0:TR, 0:TR], AX.X, ALU.max))
            link(nc.vector.tensor_scalar(q_scale[:, 1:2], q_scale[:, 0:1], 1.0 / FP8_MAX, SCALE_EPS,
                                         ALU.mult, ALU.max))
            link(nc.vector.reciprocal(q_scale[:, 2:3], q_scale[:, 1:2]))
            nc.vector.tensor_scalar(q_factor_20[:], rs, q_scale[:, 2:3], -SHIFT_20,
                                    ALU.mult, ALU.mult).then_inc(factor_ok, 1)
            nc.vector.tensor_scalar(q_factor[:], rs, q_scale[:, 2:3], -1.0,
                                    ALU.mult, ALU.mult).then_inc(factor_ok, 1)
            dve.wait_ge(factor_ok, 2)

            powers, summed = {}, {}

            def power_of_two(p):
                t, c = PIECES[p]
                dve.wait_ge(bits_ok, p + 1)
                m = xq_bits[:, t, c].bitcast(I32)
                powers[p] = mark(nc.vector.tensor_scalar(m, m, EXP_BITS, HALF_BIT, ALU.bitwise_and,
                                                         ALU.bitwise_or))

            def add_power(p):
                t, c = PIECES[p]
                dve.wait_ge(scaled_ok, p + 1)
                need(powers[p])
                summed[p] = mark(nc.vector.scalar_tensor_tensor(
                    out=y_sb[:, t, c], in0=xq_bits[:, t, c], scalar=ROUND_MIN, in1=y_sb[:, t, c],
                    op0=ALU.max, op1=ALU.add))

            def take_power(p):
                t, c = PIECES[p]
                need(summed[p])
                nc.vector.scalar_tensor_tensor(out=hn_sb[:, t, c], in0=xq_bits[:, t, c], scalar=ROUND_MIN,
                                               in1=y_sb[:, t, c], op0=ALU.max, op1=ALU.subtract,
                                               reverse1=True).then_inc(xq_ok, 1)

            def scale_first_tile(c):
                nc.vector.tensor_scalar(y_sb[:, 0, c], hn_sb[:, 0, c], q_factor[:, 0:1], None,
                                        ALU.mult).then_inc(scaled_ok, 1)

            scale_first_tile(PIECES[0][1])
            power_of_two(0)
            scale_first_tile(PIECES[1][1])
            for p in range(len(PIECES)):
                add_power(p)
                if p + 1 < len(PIECES):
                    power_of_two(p + 1)
                take_power(p)
            for t, c in RESULTS:
                dve.wait_ge(y_ps, t + 1)
                nc.vector.tensor_tensor(work_sb[:, t, c], acc[t][0:TR, c], ffn_b_row[:, c],
                                        ALU.add).then_inc(y_ok, 1)


def kernel(**inputs):
    import numpy as _np
    import concourse.bacc as _bacc
    from concourse import mybir as _mybir
    from concourse.bass_utils import run_bass_kernel_spmd as _run

    a = {k: _np.asarray(v) for k, v in inputs.items()}
    c = _np.ascontiguousarray
    x = a["x"]

    def chunked(w):
        return w.reshape(w.shape[0] // 128, 128, w.shape[1]).transpose(1, 0, 2)

    def head_in(w):
        return w.reshape(HEADS, E, KD, 128).transpose(0, 3, 2, 1).reshape(HEADS, 128, KD * E)

    heads = _np.concatenate([head_in(a["L0_attn_W_Q"]), head_in(a["L0_attn_W_K"]),
                             head_in(a["L0_attn_W_V"]), a["L0_attn_W_O"].transpose(0, 2, 1)], axis=2)
    r = _np.arange(TR)
    own = (r[:, None] // PATCHES) == (r[None, :] // PATCHES)
    later = r[None, :] > r[:, None]
    mask = _np.where(own, _np.where(later, -1e9, 0.0), -1e30).astype(_np.float32)
    tok_b = _np.zeros((B_LO + 1, D), dtype=_np.float32)
    tok_b[0] = tok_b[B_LO] = a["L0_tok_b"].reshape(D)
    arrays = {
        "patches": c(x[:, :PATCHES * 16, :]).reshape(TILES, TR, IN_DIM),
        "tok_w": c(chunked(a["L0_tok_W"])),
        "heads_w": c(heads),
        "ffn_w": c(chunked(a["L0_ffn_weight"].T)),
        "tok_g1": c(a["L0_tok_g1"].reshape(KIN, 128).T),
        "tok_b1": c(a["L0_tok_b1"].reshape(KIN, 128).T),
        "tok_b": tok_b,
        "tok_g2": a["L0_tok_g2"].reshape(1, D),
        "tok_b2": a["L0_tok_b2"].reshape(1, D),
        "ffn_scale": a["L0_ffn_weight_scale"].reshape(1, 1),
        "ffn_bias": a["L0_ffn_bias"].reshape(1, D),
        "mask": c(_np.tile(mask, (1, TILES))),
        "ident": _np.eye(128, dtype=_np.float32),
    }
    nc = _bacc.Bacc("TRN2", target_bir_lowering=False, num_devices=1)
    args = [nc.dram_tensor(n, v.shape, _mybir.dt.from_np(v.dtype), kind="ExternalInput").ap()
            for n, v in arrays.items()]
    out = nc.dram_tensor("out", (TILES, TR, D), _mybir.dt.float32, kind="ExternalOutput").ap()
    audio_tower(nc, *args, out)
    res = _run(nc, [arrays], core_ids=[0])
    return res.results[0]["out"].reshape(BATCH, PATCHES, D)
```
